# Optimizing a Trainium2 kernel written in Bass

```python
import numpy as np
import jax
import jax.numpy as jnp

def _softmax(x, axis=-1):
    return jax.nn.softmax(x, axis=axis)

def _gelu(x):
    return jax.nn.gelu(x, approximate=True)

def _silu(x):
    return jax.nn.silu(x)

def _sigmoid(x):
    return jax.nn.sigmoid(x)

def _layernorm(x, axis=-1, eps=1e-05):
    m = jnp.mean(x, axis=axis, keepdims=True)
    v = jnp.var(x, axis=axis, keepdims=True)
    return (x - m) / jnp.sqrt(v + eps)

def _scatter_add(tgt, idx, src, axis=0):
    return tgt.at[idx].add(src)

def _segment_sum(src, seg, n):
    return jax.ops.segment_sum(src, seg, n)
kernel_name = 'mk_vit_tower_d1_tok_img4096_r4_5e239b'

def setup_inputs(seed: int=0):
    np.random.seed(seed)
    _w = jnp.asarray

    def _rec_inputs():
        import jax
        import jax.numpy as jnp
        _rk = jax.random.key(seed)
        x = -0.00348982 + 0.707501 * jax.random.normal(jax.random.fold_in(_rk, 1), (16, 128, 64, 2), jnp.float32)
        return x
    x = _rec_inputs()

    def _L0_tok_setup():
        import jax, jax.numpy as jnp
        import numpy as np
        H, N, S, CH, LEN = (128, 64, 128, 1, 1024)

        def _s4d_kernel(log_dt, C, B, inv_A_real, A_imag, L):
            dt = jnp.exp(log_dt)
            Cc = C[..., 0] + 1j * C[..., 1]
            Bc = B[..., 0] + 1j * B[..., 1]
            A = -jnp.exp(inv_A_real) + 1j * A_imag
            rep = H // A.shape[0]
            A = jnp.tile(A, (rep, 1))
            Bc = jnp.tile(Bc, (rep, 1))
            dtA = A * dt[:, None]
            Cc = Bc[None, :, :] * Cc
            Cc = Cc * (jnp.exp(dtA) - 1.0) / A
            ell = jnp.arange(L, dtype=jnp.float32)
            V = jnp.exp(dtA[:, :, None] * ell)
            K = 2.0 * jnp.einsum('chn,hnl->chl', Cc, V).real
            return K.astype(jnp.float32)
        key = jax.random.key(seed)
        k1, k2 = jax.random.split(key, 2)
        log_dt = jax.random.uniform(k1, (H,), minval=float(np.log(0.001)), maxval=float(np.log(0.1))).astype(jnp.float32)
        inv_A_real = jnp.full((S, N), float(np.log(0.5)), dtype=jnp.float32)
        A_imag = jnp.tile((np.pi * jnp.arange(N, dtype=jnp.float32))[None, :], (S, 1))
        B = jnp.stack([jnp.ones((S, N), jnp.float32), jnp.zeros((S, N), jnp.float32)], axis=-1)
        C = (jax.random.normal(k2, (CH, H, N, 2)) * 0.5 ** 0.5).astype(jnp.float32)
        return {'log_dt': log_dt, 'C': C, 'B': B, 'inv_A_real': inv_A_real, 'A_imag': A_imag, 'L': LEN}
    _L0_tok_all = _L0_tok_setup()
    _L0_tok_in = {k: v for k, v in _L0_tok_all.items() if k in ('log_dt', 'B', 'inv_A_real', 'A_imag')}
    del _L0_tok_all

    def _L0_attn_setup():
        import jax, jax.numpy as jnp
        import numpy as np
        B, T, D = (1, 512, 1024)
        H, G = (32, 8)
        HD = D // H
        REP = H // G
        KV_DIM = 2 * HD * G
        key = jax.random.key(seed)
        k0, k1, k2, k3 = jax.random.split(key, 4)
        x = jax.random.normal(k0, (B, T, D), dtype=jnp.float32)
        Wq = jax.random.normal(k1, (D, D), dtype=jnp.float32) * 0.02
        Wkv = jax.random.normal(k2, (D, KV_DIM), dtype=jnp.float32) * 0.02
        Wo = jax.random.normal(k3, (D, D), dtype=jnp.float32) * 0.02
        bo = jnp.zeros((D,), dtype=jnp.float32)
        return {'x': x, 'Wq': Wq, 'Wkv': Wkv, 'Wo': Wo, 'bo': bo}
    _L0_attn_all = _L0_attn_setup()
    _L0_attn_in = {k: v for k, v in _L0_attn_all.items() if k in ('Wq', 'Wkv', 'Wo', 'bo')}
    del _L0_attn_all

    def _L0_ffn_setup():
        import jax, jax.numpy as jnp
        import numpy as np
        K_TOP = 8
        key = jax.random.key(seed)
        k1, k2, k3 = jax.random.split(key, 3)
        B, S, H, E = (4, 1024, 1024, 64)
        hidden_states = jax.random.normal(k1, (B, S, H), dtype=jnp.float32)
        router_weight = jax.random.normal(k2, (E, H), dtype=jnp.float32)
        router_bias = jnp.zeros((E,), dtype=jnp.float32)
        expert_bias = jax.random.normal(k3, (E, H), dtype=jnp.float32) * 0.1
        return {'hidden_states': hidden_states, 'router_weight': router_weight, 'router_bias': router_bias, 'expert_bias': expert_bias}
    _L0_ffn_all = _L0_ffn_setup()
    _L0_ffn_in = {k: v for k, v in _L0_ffn_all.items() if k in ('router_weight', 'router_bias', 'expert_bias')}
    del _L0_ffn_all
    return {'x': x, 'L0_tok_log_dt': _L0_tok_in['log_dt'], 'L0_tok_B': _L0_tok_in['B'], 'L0_tok_inv_A_real': _L0_tok_in['inv_A_real'], 'L0_tok_A_imag': _L0_tok_in['A_imag'], 'L0_attn_Wq': _L0_attn_in['Wq'], 'L0_attn_Wkv': _L0_attn_in['Wkv'], 'L0_attn_Wo': _L0_attn_in['Wo'], 'L0_attn_bo': _L0_attn_in['bo'], 'L0_ffn_router_weight': _L0_ffn_in['router_weight'], 'L0_ffn_router_bias': _L0_ffn_in['router_bias'], 'L0_ffn_expert_bias': _L0_ffn_in['expert_bias']}

def reference(x, L0_tok_log_dt, L0_tok_B, L0_tok_inv_A_real, L0_tok_A_imag, L0_attn_Wq, L0_attn_Wkv, L0_attn_Wo, L0_attn_bo, L0_ffn_router_weight, L0_ffn_router_bias, L0_ffn_expert_bias):
    import jax
    import jax.numpy as jnp

    def _L0_tok_ref(log_dt, C, B, inv_A_real, A_imag, L):
        import jax, jax.numpy as jnp
        import numpy as np
        H, N, S, CH, LEN = (128, 64, 128, 1, 1024)

        def _s4d_kernel(log_dt, C, B, inv_A_real, A_imag, L):
            dt = jnp.exp(log_dt)
            Cc = C[..., 0] + 1j * C[..., 1]
            Bc = B[..., 0] + 1j * B[..., 1]
            A = -jnp.exp(inv_A_real) + 1j * A_imag
            rep = H // A.shape[0]
            A = jnp.tile(A, (rep, 1))
            Bc = jnp.tile(Bc, (rep, 1))
            dtA = A * dt[:, None]
            Cc = Bc[None, :, :] * Cc
            Cc = Cc * (jnp.exp(dtA) - 1.0) / A
            ell = jnp.arange(L, dtype=jnp.float32)
            V = jnp.exp(dtA[:, :, None] * ell)
            K = 2.0 * jnp.einsum('chn,hnl->chl', Cc, V).real
            return K.astype(jnp.float32)
        return _s4d_kernel(log_dt, C, B, inv_A_real, A_imag, L)

    def _L0_attn_ref(x, Wq, Wkv, Wo, bo):
        import jax, jax.numpy as jnp
        import numpy as np
        B, T, D = (1, 512, 1024)
        H, G = (32, 8)
        HD = D // H
        REP = H // G
        KV_DIM = 2 * HD * G
        b, t, d = x.shape
        q = jnp.dot(x, Wq).reshape(b, t, H, HD).transpose(0, 2, 1, 3)
        kv = jnp.dot(x, Wkv).reshape(b, t, G, 2, HD).transpose(2, 3, 0, 1, 4)
        k, v = (kv[:, 0], kv[:, 1])
        k = jnp.broadcast_to(k[:, :, None], (G, b, REP, t, HD)).reshape(b, H, t, HD)
        v = jnp.broadcast_to(v[:, :, None], (G, b, REP, t, HD)).reshape(b, H, t, HD)
        scores = jnp.einsum('bhqd,bhkd->bhqk', q, k)
        causal = jnp.triu(jnp.ones((t, t), dtype=bool), 1)
        scores = jnp.where(causal[None, None], -jnp.inf, scores)
        weights = jax.nn.softmax(scores * (1.0 / HD ** 0.5), axis=-1)
        ctx = jnp.einsum('bhqk,bhkd->bhqd', weights, v)
        ctx = ctx.transpose(0, 2, 1, 3).reshape(b, t, d)
        return jnp.dot(ctx, Wo) + bo

    def _L0_ffn_ref(hidden_states, router_weight, router_bias, expert_bias):
        import jax, jax.numpy as jnp
        import numpy as np
        K_TOP = 8
        B, S, H = hidden_states.shape
        E = router_weight.shape[0]
        T = B * S
        flat = hidden_states.reshape(T, H)
        logits = jnp.einsum('th,eh->te', flat, router_weight) + router_bias
        scores = jax.nn.softmax(logits, axis=-1)
        topk_w, topk_idx = jax.lax.top_k(scores, K_TOP)
        w_sum = topk_w.sum(axis=-1, keepdims=True)
        w_dense = jnp.zeros((T, E), dtype=scores.dtype).at[jnp.arange(T)[:, None], topk_idx].add(topk_w)
        bias_mix = jnp.einsum('te,eh->th', w_dense, expert_bias)
        out = flat * w_sum + bias_mix
        return out.reshape(B, S, H)
    h = _L0_tok_ref(L0_tok_log_dt, x, L0_tok_B, L0_tok_inv_A_real, L0_tok_A_imag, 1024)
    h = h + _L0_attn_ref(_layernorm(h, axis=-1), L0_attn_Wq, L0_attn_Wkv, L0_attn_Wo, L0_attn_bo)
    h = h + _L0_ffn_ref(_layernorm(h, axis=-1), L0_ffn_router_weight, L0_ffn_router_bias, L0_ffn_expert_bias)
    return h

_drawn_inputs = setup_inputs


def setup_inputs(seed=0):
    import zlib

    import numpy as np

    out = dict(_drawn_inputs(seed))
    spreads = {'L0_tok_inv_A_real': (-0.6931471824645996, 0.2),
     'L0_attn_bo': (0.0, 0.1),
     'L0_ffn_router_bias': (0.0, 0.1)}
    factors = {}
    for name, (base, spread) in spreads.items():
        noise = np.random.default_rng([zlib.crc32(name.encode()), seed]).standard_normal(out[name].shape)
        drawn = base * np.exp(spread * noise) if base else spread * noise
        out[name] = jnp.asarray(drawn.astype(out[name].dtype))
    for name, factor in factors.items():
        out[name] = (out[name] * factor).astype(out[name].dtype)
    return out
```

```python
import numpy as np
import concourse.bass as bass
from concourse import mybir
from contextlib import ExitStack

F32 = mybir.dt.float32
F32R = mybir.dt.float32r
BF16 = mybir.dt.bfloat16
I32 = mybir.dt.int32
ALU = mybir.AluOpType
ACT = mybir.ActivationFunctionType
AX = mybir.AxisListType

P = 128
BATCH, T, D = 16, 128, 1024
MODES = 64
L0, L1 = 8, 128
LA, LB = 8, 16
NSTEP = L0 + LA + LB
J_ONE = L0 + LA + 1
KD = D // P
NH, NG, HD = 32, 8, 32
REP = NH // NG
GG = 2
GJ = NG // GG
SB = 4
NE, TOPK = 64, 8
EPS = 1e-5
SCALE = 1.0 / HD ** 0.5
NEG = -1e30
LOWEST = -3e38

HG = 8
NGRP = T // HG
TWO_PI = 2.0 * np.pi
C1 = 6.28125
C2 = float(np.float32(round((TWO_PI - C1) * 2 ** 20) / 2 ** 20))
C3 = float(np.float32(TWO_PI - C1 - C2))
PI_IN = 3.1415925
ROUND = 1.5 * 2.0 ** 23
RSQRT_MAGIC = float(0x5F3759DF)


def bcast(ap, axis, n):
    a = ap.unsqueeze(axis)
    shape = list(a.shape)
    shape[axis] = n
    return a.broadcast_to(shape)


class Chain:

    def __init__(self, eng, sem, base=0):
        self.eng, self.sem, self.base, self.k = eng, sem, base, 0

    def mark(self, ins):
        ins.then_inc(self.sem, 1)
        self.k += 1

    def wait(self):
        self.eng.wait_ge(self.sem, self.base + self.k)

    def link(self, ins):
        self.mark(ins)
        self.wait()


def build(nc, c_re_im, log_dt, b_re_im, inv_a, a_imag, w_qkv, w_out, bo, router_t, rbias, ebias, out):
    x_scr = nc.dram_tensor("x_scratch", (BATCH * L0, T, L1), F32, kind="Internal").ap()
    q_scr = nc.dram_tensor("q_scratch", (BATCH, P, GG * REP, P), F32, kind="Internal").ap()
    k_scr = nc.dram_tensor("k_scratch", (NG, GJ * HD, BATCH // SB, P), F32, kind="Internal").ap()

    es = ExitStack()
    with es:
        def sb(name, shape, dt=F32, stack=es):
            return stack.enter_context(nc.sbuf_tensor(name, shape, dt))

        def sem(name):
            return es.enter_context(nc.semaphore(name))

        w_hi = sb("w_hi", [P, KD, D], F32R)
        w_lo = sb("w_lo", [P, KD, D], F32R)
        w_stage = sb("w_stage", [P, D])
        ident = sb("ident", [P, P])
        ident_bf = sb("ident_bf", [P, P], BF16)
        above_bf = sb("above_bf", [P, REP, P], BF16)
        ones32 = sb("ones32", [P, HD])
        steps = sb("steps", [P, NSTEP])
        steps_i = sb("steps_i", [P, NSTEP], I32)
        half_pi = sb("half_pi", [P, 1])
        carrier = sb("carrier", [P, 2])
        in_group = sb("in_group", [P, NG])
        in_place = sb("in_place", [P, REP])
        group_sel = sb("group_sel", [P, NG, P], F32R)

        eab = ExitStack()
        kv_hi = sb("kv_hi", [P, KD // 2, D], F32R, stack=eab)
        kv_lo = sb("kv_lo", [P, KD // 2, D], F32R, stack=eab)

        ea = ExitStack()
        e_re = sb("e_re", [P, T, NSTEP], stack=ea)
        e_im = sb("e_im", [P, T, NSTEP], stack=ea)
        a1 = sb("a1", [P, T, LA], stack=ea)
        a2 = sb("a2", [P, T, LA], stack=ea)
        g1 = sb("g1", [P, T, L0], stack=ea)
        g2 = sb("g2", [P, T, L0], stack=ea)
        c_re = sb("c_re", [P, T, BATCH], stack=ea)
        c_im = sb("c_im", [P, T, BATCH], stack=ea)
        work = sb("work", [P, 9, D], stack=ea)
        th = work[:, 0:4, :].rearrange("p a (b j) -> p (a b) j", j=NSTEP)
        kk = work[:, 4:8, :].rearrange("p a (b j) -> p (a b) j", j=NSTEP)
        e1_slot = [work[:, 0, :], work[:, 1, :]]
        p1_slot = [work[:, 2, :], work[:, 3, :]]
        p2_slot = [work[:, 4, :], work[:, 5, :]]
        t2_tmp = work[:, 6, :]
        x_stage = [work[:, 7, :], work[:, 8, :]]
        names = ["ldt", "inva", "aim", "bre", "bim", "dt", "em", "ar", "ai", "sh", "tnh", "q2", "xr",
                 "den", "ni", "nr", "yr", "yi", "fr", "fi", "nfr", "m"]
        room = [t.rearrange("p (n t) -> p n t", t=T) for t in
                (work[:, 8, :], g1[:, :, :].rearrange("p t l -> p (t l)"),
                 g2[:, :, :].rearrange("p t l -> p (t l)"))]
        sm = {n: room[k // L0][:, k % L0, :] for k, n in enumerate(names)}
        ea.close()

        eb = ExitStack()
        v_all = sb("v_all", [P, BATCH, NG * HD], stack=eb)
        x_tok = [sb(f"x_tok{n}", [P, D], stack=eb) for n in range(SB)]
        xt_hi = sb("xt_hi", [P, KD, SB * P], F32R, stack=eb)
        xt_lo = sb("xt_lo", [P, KD, SB * P], F32R, stack=eb)
        qk_stage = [sb(f"qk_stage{n}", [P, SB * P], stack=eb) for n in range(4)]
        bst = sb("bst", [P, SB, 12], stack=eb)
        bmv = sb("bmv", [P, SB, 2], stack=eb)
        bvr = sb("bvr", [P, 4, SB], stack=eb)
        eb.close()
        eab.close()

        ec = ExitStack()
        p_t = [sb(f"p_t{n}", [P, GJ, REP * P], stack=ec) for n in range(2)]
        o_hi = [sb(f"o_hi{n}", [P, D], F32R, stack=ec) for n in range(2)]
        o_lo = [sb(f"o_lo{n}", [P, D], F32R, stack=ec) for n in range(2)]
        sb("v_all_place", [P, BATCH, NG * HD], stack=ec)
        q_t = [sb(f"q_t{n}", [P, GG * REP, P], stack=ec) for n in range(2)]
        q_bf = [sb(f"q_bf{n}", [P, GG * REP, P], BF16, stack=ec) for n in range(2)]
        k_t = [sb(f"k_t{n}", [P, GG, P], stack=ec) for n in range(2)]
        k_bf = [sb(f"k_bf{n}", [P, GG, P], BF16, stack=ec) for n in range(2)]
        v_tok = [sb(f"v_tok{n}", [P, NG, HD], stack=ec) for n in range(2)]
        o_t = [sb(f"o_t{n}", [P, D], stack=ec) for n in range(2)]
        rsum = [sb(f"rsum{n}", [P, REP * P], stack=ec) for n in range(2)]
        shift = [sb(f"shift{n}", [P, REP, P], F32R, stack=ec) for n in range(2)]
        row_max = [sb(f"row_max{n}", [P, 4, NH], stack=ec) for n in range(2)]
        x_res = [sb(f"x_res{n}", [P, D], stack=ec) for n in range(2)]
        h2 = [sb(f"h2_{n}", [P, D], stack=ec) for n in range(2)]
        hn = sb("hn", [P, D], stack=ec)
        hn_t = sb("hn_t", [P, KD, P], stack=ec)
        y_out = [sb(f"y_out{n}", [P, D], stack=ec) for n in range(2)]
        rw = sb("rw", [P, KD, NE], stack=ec)
        rb_all = sb("rb_all", [P, NE], stack=ec)
        eb_one = sb("eb_one", [NE + 1, D], stack=ec)
        bo_all = sb("bo_all", [P, D], stack=ec)
        cst = sb("cst", [P, 12], stack=ec)
        cmv = sb("cmv", [P, 2], stack=ec)
        cvr = sb("cvr", [P, 4], stack=ec)
        rstd2 = [sb(f"rstd2_{n}", [P, 1], stack=ec) for n in range(2)]
        nmr2 = [sb(f"nmr2_{n}", [P, 1], stack=ec) for n in range(2)]
        logit = sb("logit", [P, NE], stack=ec)
        ranked = sb("ranked", [P, TOPK], stack=ec)
        struck = sb("struck", [P, NE], stack=ec)
        neg_top = sb("neg_top", [P, 1], stack=ec)
        expd = sb("expd", [P, NE], stack=ec)
        zsum = sb("zsum", [P, 1], stack=ec)
        chosen = sb("chosen", [P, NE], stack=ec)
        wsum = sb("wsum", [P, 1], stack=ec)
        rz = sb("rz", [P, 1], stack=ec)
        w_aug = sb("w_aug", [P, NE + 1], stack=ec)
        w_aug_t = sb("w_aug_t", [NE + 1, P], stack=ec)
        hscale = [sb(f"hscale{n}", [P, 1], stack=ec) for n in range(2)]
        ec.close()

        bank = [es.enter_context(nc.psum_tensor(f"bank{n}", [P, 512], F32)) for n in range(8)]

        s_par = sem("s_par")
        s_c = sem("s_c")
        s_const = sem("s_const")
        s_steps = sem("s_steps")
        s_dt = sem("s_dt")
        s_angle = sem("s_angle")
        s_trig = sem("s_trig")
        s_decay = sem("s_decay")
        s_mag = sem("s_mag")
        s_etab = sem("s_etab")
        s_atab = sem("s_atab")
        s_wload = sem("s_wload")
        s_whi = sem("s_whi")
        s_wlo = sem("s_wlo")
        s_fac = sem("s_fac")
        s_xmm = sem("s_xmm")
        s_xev = sem("s_xev")
        s_xst = [sem(f"s_xst{n}") for n in range(2)]
        s_dve = sem("s_dve")
        s_xld = [sem(f"s_xld{n}") for n in range(SB)]
        s_xn = sem("s_xn")
        s_tp = sem("s_tp")
        s_thi = sem("s_thi")
        s_tlo = sem("s_tlo")
        s_pj = sem("s_pj")
        s_pja = sem("s_pja")
        s_qst = [sem(f"s_qst{n}") for n in range(4)]
        s_tab = sem("s_tab")
        s_wol = [sem(f"s_wol{n}") for n in range(2)]
        s_qk = [sem(f"s_qk{n}") for n in range(2)]
        s_rld = [sem(f"s_rld{n}") for n in range(2)]
        s_cast = sem("s_cast")
        s_sq = sem("s_sq")
        s_mx = sem("s_mx")
        s_mc = sem("s_mc")
        s_mt = sem("s_mt")
        s_sh = sem("s_sh")
        s_sk = sem("s_sk")
        s_pe = sem("s_pe")
        s_msk = sem("s_msk")
        s_pv = sem("s_pv")
        s_nrm = sem("s_nrm")
        s_ohi = sem("s_ohi")
        s_olo = sem("s_olo")
        s_xb = sem("s_xb")
        s_y = sem("s_y")
        s_h2 = sem("s_h2")
        s_hn = sem("s_hn")
        s_ht = sem("s_ht")
        s_hte = sem("s_hte")
        s_rt = sem("s_rt")
        s_lg = sem("s_lg")
        s_ex = sem("s_ex")
        s_wa = sem("s_wa")
        s_wt = sem("s_wt")
        s_wte = sem("s_wte")
        s_mix = sem("s_mix")
        s_fin = sem("s_fin")
        s_out = [sem(f"s_out{n}") for n in range(2)]
        s_ones = sem("s_ones")

        s_kst = sem("s_kst")
        Q_STORES = [sum(1 for t in range(10) if t % 4 == n) for n in range(4)]
        TBANK = [0, 1, 6, 7]
        N_CONST = 8

        def after(eng, semaphore, count):
            if not (isinstance(count, int) and count <= 0):
                eng.wait_ge(semaphore, count)

        STEADY = 3
        N_STEADY = (BATCH - 1 - STEADY) // 2

        def steps_of_c(eng, step):
            for b in range(-1, STEADY):
                step(b, b % 2)
            with eng.Fori(0, N_STEADY) as pr:
                for u in range(2):
                    step(pr * 2 + (STEADY + u), (STEADY + u) % 2)
            for b in range(BATCH - 1, BATCH + 3):
                step(b, b % 2)

        def has(b):
            return not isinstance(b, int) or 0 <= b < BATCH

        def carry_dve():
            nc.vector.tensor_copy(carrier[:, 0:1], ones32[:, 0:1])

        def carry_pool():
            nc.gpsimd.tensor_tensor(carrier[:, 1:2], ones32[:, 0:1], ones32[:, 0:1], ALU.mult)

        block = es.enter_context(nc.Block())

        @block.sync
        def _(sp):
            sp.dma_start(sm["ldt"][:, :], log_dt.rearrange("(a h) -> a h", a=1).broadcast_to([P, T]))\
              .then_inc(s_par, 16)
            for half in (0, MODES):
                rows = slice(half, half + MODES)
                sp.dma_start(sm["inva"][rows, :], inv_a).then_inc(s_par, 16)
                sp.dma_start(sm["aim"][rows, :], a_imag).then_inc(s_par, 16)
                sp.dma_start(sm["bre"][rows, :], b_re_im[0]).then_inc(s_par, 16)
                sp.dma_start(sm["bim"][rows, :], b_re_im[1]).then_inc(s_par, 16)
            for k in range(8, 12):
                if k > 8:
                    sp.wait_ge(s_whi, k - 8)
                    sp.wait_ge(s_wlo, k - 8)
                sp.dma_start(w_stage[:, :], w_qkv[k]).then_inc(s_wload, 16)
                if k == 8:
                    for half in (0, MODES):
                        rows = slice(half, half + MODES)
                        sp.dma_start(c_re[rows, :, :], c_re_im[0]).then_inc(s_c, 16)
                        sp.dma_start(c_im[rows, :, :], c_re_im[1]).then_inc(s_c, 16)
            for u in range(2):
                sp.sem_inc(s_xst[u], 16)
                sp.sem_inc(s_out[u], 16)
            with sp.Fori(0, NGRP // 2) as it:
                sp.wait_ge(s_whi, it + 4)
                sp.wait_ge(s_wlo, it + 4)
                sp.dma_start(w_stage[:, :], w_qkv[it]).then_inc(s_wload, 16)
                for u in range(2):
                    sp.wait_ge(s_xev, it * 4 + 2 * u + 5)
                    sp.dma_start(x_scr[:, bass.ds(it * (2 * HG) + u * HG, HG), :],
                                 x_stage[u].rearrange("p (h l) -> p h l", h=HG)).then_inc(s_xst[u], 16)
            for n in range(4):
                sp.sem_inc(s_qst[n], 16)
            with sp.Fori(0, BATCH // SB) as i:
                for t in range(GG + GG * REP):
                    sp.wait_ge(s_pja, i * 14 + t + 1)
                    src = qk_stage[t % 4][:, :].rearrange("p (s t) -> p s t", s=SB)
                    if t < GG:
                        for g in range(GJ):
                            sp.dma_start(k_scr[t * GJ + g].rearrange("(j w) i k -> w j i k", j=GJ)
                                         [:, :, bass.ds(i, 1), :],
                                         src[g * HD:(g + 1) * HD, :, :].unsqueeze(2))\
                              .then_inc(s_kst if g < GJ - 1 else s_qst[t % 4], 16)
                    else:
                        sp.dma_start(q_scr[bass.ds(i * SB, SB), :, t - GG, :].rearrange("s p t -> p s t"),
                                     src).then_inc(s_qst[t % 4], 16)
            for n in range(4):
                sp.wait_ge(s_qst[n], 16 * (1 + Q_STORES[n] * (BATCH // SB)))
            sp.wait_ge(s_kst, 16 * (GJ - 1) * GG * (BATCH // SB))

            def load_qk(b, slot, group):
                after(sp, s_sk, b * 8 - 8)
                sp.dma_start(q_t[slot][:, :, :], q_scr[b]).then_inc(s_qk[slot], 16)
                sp.dma_start(k_t[slot][:, :, :], k_scr[group][:, slot * GG:(slot + 1) * GG, :])\
                  .then_inc(s_qk[slot], 16)

            x_rows = x_scr.rearrange("(b m) t l -> b t m l", b=BATCH)

            def load_res(b, slot):
                after(sp, s_h2, b - 1)
                sp.dma_start(x_res[slot][:, :].rearrange("p (m l) -> p m l", m=L0), x_rows[b])\
                  .then_inc(s_rld[slot], 16)

            for b in range(2):
                load_qk(b, b, 0)
            for k in range(KD):
                if k >= 2:
                    sp.wait_ge(s_whi, 12 + k - 1)
                    sp.wait_ge(s_wlo, 12 + k - 1)
                sp.dma_start(y_out[k % 2][:, :], w_out[k]).then_inc(s_wol[k % 2], 16)
            sp.dma_start(bo_all[:, :], bo.rearrange("(a e) -> a e", a=1).broadcast_to([P, D]))\
              .then_inc(s_tab, 16)
            sp.dma_start(rw[:, :, :], router_t.rearrange("(k p) e -> p k e", p=P)).then_inc(s_tab, 16)
            sp.dma_start(rb_all[:, :], rbias.rearrange("(a e) -> a e", a=1).broadcast_to([P, NE]))\
              .then_inc(s_tab, 16)
            sp.dma_start(eb_one[0:NE, :], ebias).then_inc(s_tab, 16)
            load_res(0, 0)

            def step(b, slot):
                if has(b - 3):
                    sp.wait_ge(s_fin, b - 2)
                    sp.dma_start(out[b - 3], y_out[1 - slot][:, :]).then_inc(s_out[1 - slot], 16)
                if isinstance(b, int):
                    if 0 <= b < BATCH - 2:
                        load_qk(b + 2, slot, (b + 2) // 2)
                    if 0 <= b < BATCH - 1:
                        load_res(b + 1, 1 - slot)
                else:
                    load_qk(b + 2, slot, group_of[0])
                    load_res(b + 1, 1 - slot)

            group_of = [None]

            for b in range(-1, STEADY):
                step(b, b % 2)
            with sp.Fori(0, N_STEADY - 1) as pr:
                for u in range(2):
                    group_of[0] = pr + (STEADY + u + 2) // 2
                    step(pr * 2 + (STEADY + u), (STEADY + u) % 2)
            for b in range(STEADY + 2 * (N_STEADY - 1), BATCH + 3):
                step(b, b % 2)
            for u in range(2):
                sp.wait_ge(s_out[u], 16 * (BATCH // 2 + 1))

        @block.gpsimd
        def _(pool):
            g = nc.gpsimd
            g.iota(steps_i[:, 0:L0], pattern=[[P, L0]], base=0, channel_multiplier=0).then_inc(s_steps, 1)
            g.iota(steps_i[:, L0:L0 + LA], pattern=[[LB, LA]], base=0, channel_multiplier=0).then_inc(s_steps, 1)
            g.iota(steps_i[:, L0 + LA:NSTEP], pattern=[[1, LB]], base=0, channel_multiplier=0)\
             .then_inc(s_steps, 1)
            g.memset(half_pi[:, :], float(np.pi / 2)).then_inc(s_const, 1)
            g.memset(ident[:, :], 0.0).then_inc(s_const, 1)
            g.memset(ident_bf[:, :], 0.0).then_inc(s_const, 1)
            g.memset(above_bf[:, :, :], 0.0).then_inc(s_const, 1)
            g.memset(ones32[:, :], 1.0).then_inc(s_const, 1)
            pool.wait_ge(s_const, 5)
            for m in (ident, ident_bf):
                g.affine_select(out=m[:, :], in_=m[:, :], compare_op=ALU.not_equal, fill=1.0, base=0,
                                pattern=[[-1, P]], channel_multiplier=1).then_inc(s_const, 1)
            g.affine_select(out=above_bf[:, :, :], in_=above_bf[:, :, :], compare_op=ALU.is_ge, fill=NEG,
                            base=0, pattern=[[0, REP], [-1, P]], channel_multiplier=1).then_inc(s_const, 1)
            for u in range(2):
                pool.wait_ge(s_xst[u], 16 * (NGRP // 2 + 1))
            x_rows = x_scr.rearrange("(b m) t l -> b t m l", b=BATCH)
            with pool.Fori(0, BATCH // SB) as i:
                for b in range(SB):
                    pool.wait_ge(s_tp, i * (2 * SB) + 2 * b + 2)
                    pool.dma_start(x_tok[b][:, :].rearrange("p (m l) -> p m l", m=L0), x_rows[i * SB + b])\
                        .then_inc(s_xld[b], 16)
            pool.sem_inc(s_msk, 1)
            for n in range(4):
                pool.wait_ge(s_qst[n], 16 * (1 + Q_STORES[n] * (BATCH // SB)))
            g.memset(eb_one[NE:NE + 1, :], 1.0).then_inc(s_ones, 1)
            pool.wait_ge(s_ones, 1)
            pool.wait_ge(s_tab, 64)
            with pool.Fori(0, BATCH // 2) as it:
                for u in range(2):
                    for gg in range(GG):
                        b8 = it * 16 + 8 * u
                        pool.wait_ge(s_pe, b8 + GJ * (gg + 1))
                        pool.wait_ge(s_msk, it * 4 + 2 * u + gg + 1)
                        carry_pool()
                        view = p_t[gg][:, :, :].rearrange("p j (r q) -> p (j r) q", r=REP)
                        g.affine_select(out=view, in_=view, compare_op=ALU.is_ge, fill=0.0, base=0,
                                        pattern=[[0, GJ * REP], [1, P]], channel_multiplier=-1)\
                         .then_inc(s_msk, 1)
                    pool.wait_ge(s_rld[u], it * 16 + 16)
                    pool.wait_ge(s_msk, it * 4 + 2 * u + 3)
                    g.tensor_tensor(x_res[u][:, :], x_res[u][:, :], bo_all[:, :], ALU.add)\
                     .then_inc(s_xb, 1)

        @block.scalar
        def _(act):
            a = nc.scalar
            act.sem_inc(s_xev, 3)
            act.wait_ge(s_par, 9 * 16)
            a.activation(sm["dt"][:, :], sm["ldt"][:, :], ACT.Exp).then_inc(s_dt, 1)
            a.activation(sm["em"][:, :], sm["inva"][:, :], ACT.Exp).then_inc(s_dt, 1)

            for k in range(KD // 2):
                act.wait_ge(s_wload, 16 * (k + 1))
                a.activation(kv_hi[:, k, :], w_stage[:, :], ACT.Copy).then_inc(s_whi, 1)
            act.wait_ge(s_angle, 1)
            a.activation(e_im[:, :, :], th, ACT.Sin).then_inc(s_trig, 1)
            a.activation(sm["sh"][:, :], th[:, :, J_ONE], ACT.Sin, scale=0.5).then_inc(s_trig, 1)
            act.wait_ge(s_angle, 2)
            act.wait_ge(s_const, 1)
            a.activation(e_re[:, :, :], kk, ACT.Sin, bias=half_pi[:, 0:1]).then_inc(s_trig, 1)
            act.wait_ge(s_trig, 3)
            act.wait_ge(s_decay, 1)
            a.activation(kk, th, ACT.Exp).then_inc(s_mag, 1)
            a.activation(sm["tnh"][:, :], sm["ar"][:, :], ACT.Tanh, scale=0.5).then_inc(s_mag, 1)
            act.wait_ge(s_etab, 1)
            top, bot = slice(0, MODES), slice(MODES, P)
            cols = slice(L0, L0 + LA)
            a.activation(a1[top, :, :], e_re[top, :, cols], ACT.Copy).then_inc(s_atab, 1)
            a.activation(a2[top, :, :], e_im[top, :, cols], ACT.Copy, scale=-1.0).then_inc(s_atab, 1)
            a.activation(a1[bot, :, :], e_im[bot, :, cols], ACT.Copy).then_inc(s_atab, 1)
            a.activation(a2[bot, :, :], e_re[bot, :, cols], ACT.Copy).then_inc(s_atab, 1)
            with act.Fori(0, NGRP // 2) as it:
                act.wait_ge(s_wload, it * 16 + 5 * 16)
                a.activation(w_hi[:, bass.ds(it, 1), :], w_stage[:, :].unsqueeze(1), ACT.Copy)\
                 .then_inc(s_whi, 1)
                for u in range(2):
                    act.wait_ge(s_xst[u], it * 16 + 16)
                    for n in range(2):
                        act.wait_ge(s_xmm, it * 4 + 2 * u + n + 4)
                        a.activation(x_stage[u][:, n * 512:(n + 1) * 512], bank[2 * u + n][:, :], ACT.Copy)\
                         .then_inc(s_xev, 1)

            with act.Fori(0, BATCH // SB) as i:
                act.wait_ge(s_pj, i * 14 + 1)
                for n in range(2 * SB):
                    b, half = n // 2, n % 2
                    act.wait_ge(s_tp, i * (2 * SB) + n + 9)
                    a.activation(xt_hi[:, half * 4:half * 4 + 4, b * P:(b + 1) * P],
                                 bank[TBANK[n % 4]][:, :].rearrange("p (k t) -> p k t", k=4), ACT.Copy)\
                     .then_inc(s_thi, 1)
                stores = [0] * 4
                for t in range(14):
                    act.wait_ge(s_pj, i * 14 + t + 2)
                    src = bank[2 + t % 4]
                    if t < 10:
                        act.wait_ge(s_qst[t % 4], i * (16 * Q_STORES[t % 4]) + 16 * (stores[t % 4] + 1))
                        stores[t % 4] += 1
                        if t in (4, 5):
                            act.wait_ge(s_kst, i * (16 * (GJ - 1) * GG) + 16 * (GJ - 1) * (t - 3))
                        a.activation(qk_stage[t % 4][:, :], src[:, :], ACT.Copy).then_inc(s_pja, 1)
                    else:
                        a.activation(v_all[:, bass.ds(i * SB + (t - 10), 1), :],
                                     src[:, 0:NG * HD].unsqueeze(1), ACT.Copy).then_inc(s_pja, 1)

            def cast(b, slot, group):
                after(act, s_sq, b * 8 - 8)
                after(act, s_pv, b * 2 - 2)
                act.wait_ge(s_qk[slot], group * 32 + 32)
                a.activation(q_bf[slot][:, :, :], q_t[slot][:, :, :], ACT.Copy)
                a.activation(k_bf[slot][:, :, :], k_t[slot][:, :, :], ACT.Copy)
                cols = slice(group * HD, (group + 1) * HD) if isinstance(group, int) else \
                    bass.ds(group * HD, HD)
                a.activation(v_tok[slot][:, :, :], v_all[:, slot * NG:(slot + 1) * NG, cols], ACT.Copy)\
                 .then_inc(s_cast, 1)

            def exponentials(b, gg):
                after(act, s_pv, b * 2 - 1 + gg)
                for j in range(GJ):
                    act.wait_ge(s_sk, b * 8 + gg * GJ + j + 1)
                    a.activation(p_t[gg][:, j, :], bank[4 + j % 2][:, :], ACT.Exp, scale=SCALE)\
                     .then_inc(s_pe, 1)

            def context_hi(b, slot, gg):
                act.wait_ge(s_nrm, b * 2 + gg + 1)
                after(act, s_y, b * 2 - 2)
                cols = slice(gg * 512, (gg + 1) * 512)
                a.activation(o_hi[slot][:, cols], o_t[slot][:, cols], ACT.Copy).then_inc(s_ohi, 1)

            def step(b, slot, group=None):
                if has(b - 3):
                    act.wait_ge(s_wt, b - 2)
                    a.activation(w_aug_t[:, :], bank[4][0:NE + 1, 0:P], ACT.Copy).then_inc(s_wte, 1)
                if has(b):
                    exponentials(b, 0)
                if isinstance(b, int) and b == -1:
                    cast(0, 0, 0)
                    for k in range(KD):
                        act.wait_ge(s_wol[k % 2], 16 * (k // 2 + 1))
                        a.activation(w_hi[:, k, :], y_out[k % 2][:, :], ACT.Copy).then_inc(s_whi, 1)
                if has(b - 1):
                    context_hi(b - 1, 1 - slot, 1)
                if has(b):
                    context_hi(b, slot, 0)
                if has(b - 2):
                    for half in range(2):
                        act.wait_ge(s_ht, b * 2 + half - 3)
                        a.activation(hn_t[:, half * 4:half * 4 + 4, :],
                                     bank[2 + half][:, :].rearrange("p (k t) -> p k t", k=4), ACT.Copy)\
                         .then_inc(s_hte, 1)
                if has(b):
                    exponentials(b, 1)
                if has(b - 2):
                    act.wait_ge(s_lg, b - 1)
                    a.activation(expd[:, :], logit[:, :], ACT.Exp, bias=neg_top[:, 0:1],
                                 accum_out=zsum[:, 0:1]).then_inc(s_ex, 1)
                if isinstance(b, int):
                    if b + 2 < BATCH:
                        cast(b + 2, slot, (b + 2) // 2)
                else:
                    cast(b + 2, slot, group)

            for b in range(-1, STEADY):
                step(b, b % 2)
            with act.Fori(0, N_STEADY - 1) as pr:
                for u in range(2):
                    step(pr * 2 + (STEADY + u), (STEADY + u) % 2, pr + (STEADY + u + 2) // 2)
            for b in range(STEADY + 2 * (N_STEADY - 1), BATCH + 3):
                step(b, b % 2)

        @block.vector
        def _(dve):
            v = nc.vector
            dve.sem_inc(s_fac, 2)
            dve.sem_inc(s_tlo, 4)
            ch = Chain(dve, s_dve)
            tt, stt, ts = v.tensor_tensor, v.scalar_tensor_tensor, v.tensor_scalar
            s = {n: t[:, :] for n, t in sm.items()}
            dve.wait_ge(s_steps, 3)
            ch.mark(v.tensor_copy(steps[:, :], steps_i[:, :]))
            dve.wait_ge(s_dt, 2)
            ch.mark(stt(s["ar"], s["em"], -1.0, s["dt"], ALU.mult, ALU.mult))
            ch.link(tt(s["ai"], s["aim"], s["dt"], ALU.mult))
            st_b = bcast(steps[:, :], 1, T)
            ch.link(tt(th, bcast(s["ai"], 2, NSTEP), st_b, ALU.mult))
            ch.link(ts(kk, th, float(1.0 / TWO_PI), ROUND, ALU.mult, ALU.add))
            ch.link(ts(kk, kk, ROUND, None, ALU.subtract))
            for c in (C1, C2, C3):
                ch.link(stt(th, kk, -c, th, ALU.mult, ALU.add))
            ts(th, th, PI_IN, -PI_IN, ALU.min, ALU.max).then_inc(s_angle, 1)
            dve.wait_ge(s_angle, 1)
            stt(kk, th, -1.0, th, ALU.mult, ALU.min).then_inc(s_angle, 1)

            def w_low(dst, chunk, high):
                tt(dst, chunk, high, ALU.subtract).then_inc(s_wlo, 1)

            for k in range(KD // 2):
                dve.wait_ge(s_whi, k + 1)
                w_low(kv_lo[:, k, :], w_stage[:, :], kv_hi[:, k, :].bitcast(F32))
            ch.mark(tt(s["den"], s["em"], s["em"], ALU.mult))
            ch.link(tt(s["m"], s["aim"], s["aim"], ALU.mult))
            ch.link(tt(s["den"], s["den"], s["m"], ALU.add))
            ch.link(v.reciprocal(s["den"], s["den"]))
            ch.mark(stt(s["nr"], s["em"], -2.0, s["den"], ALU.mult, ALU.mult))
            ch.mark(stt(s["ni"], s["aim"], -2.0, s["den"], ALU.mult, ALU.mult))
            dve.wait_ge(s_trig, 2)
            tt(th, bcast(s["ar"], 2, NSTEP), st_b, ALU.mult).then_inc(s_decay, 1)
            ch.link(stt(s["q2"], s["sh"], 2.0, s["sh"], ALU.mult, ALU.mult))
            ch.mark(ts(s["m"], s["q2"], -1.0, 1.0, ALU.mult, ALU.add))
            dve.wait_ge(s_mag, 2)
            ch.link(stt(s["xr"], kk[:, :, J_ONE], 1.0, s["tnh"], ALU.add, ALU.mult))
            ch.link(tt(s["xr"], s["xr"], s["m"], ALU.mult))
            ch.mark(tt(s["xr"], s["xr"], s["q2"], ALU.subtract))
            dve.wait_ge(s_trig, 3)
            tt(e_re[:, :, :], e_re[:, :, :], kk, ALU.mult).then_inc(s_dve, 1)
            ch.k += 1
            ch.link(tt(e_im[:, :, :], e_im[:, :, :], kk, ALU.mult))
            v.tensor_copy(s["sh"], e_im[:, :, J_ONE]).then_inc(s_etab, 1)
            dve.wait_ge(s_etab, 1)
            xi = s["sh"]

            def cmul(zr, zi, ar_, ai_, br_, bi_, t):
                ch.mark(tt(zr, ar_, br_, ALU.mult))
                ch.link(tt(t, ai_, bi_, ALU.mult))
                ch.mark(tt(zr, zr, t, ALU.subtract))
                ch.link(tt(zi, ar_, bi_, ALU.mult))
                ch.link(tt(t, ai_, br_, ALU.mult))
                ch.link(tt(zi, zi, t, ALU.add))

            cmul(s["yr"], s["yi"], s["xr"], xi, s["nr"], s["ni"], s["m"])
            cmul(s["fr"], s["fi"], s["yr"], s["yi"], s["bre"], s["bim"], s["m"])
            ch.mark(ts(s["nfr"], s["fr"], -1.0, None, ALU.mult))
            ch.wait()
            z = [work[:, n, :].rearrange("p (h l) -> p h l", l=L0) for n in range(4)]
            e0r, e0i = e_re[:, :, 0:L0], e_im[:, :, 0:L0]
            ch.mark(tt(z[0], bcast(s["fr"], 2, L0), e0r, ALU.mult))
            ch.mark(tt(z[1], bcast(s["fi"], 2, L0), e0i, ALU.mult))
            ch.mark(tt(z[2], bcast(s["nfr"], 2, L0), e0i, ALU.mult))
            ch.link(tt(z[3], bcast(s["fi"], 2, L0), e0r, ALU.mult))
            top, bot = slice(0, MODES), slice(MODES, P)
            ch.mark(tt(g1[top, :, :], z[0][top], z[1][top], ALU.subtract))
            ch.mark(tt(g2[top, :, :], z[2][top], z[3][top], ALU.subtract))
            ch.mark(tt(g1[bot, :, :], z[2][bot], z[3][bot], ALU.subtract))
            ch.link(tt(g2[bot, :, :], z[1][bot], z[0][bot], ALU.subtract))
            dve.wait_ge(s_atab, 4)
            dve.wait_ge(s_c, 64)

            base = ch.k
            with dve.Fori(0, NGRP // 2) as it:
                lc = Chain(dve, s_dve, it * 6 + base)
                for u in range(2):
                    hs = bass.ds(it * (2 * HG) + u * HG, HG)
                    dve.wait_ge(s_xmm, it * 4 + 2 * u + 1)
                    dve.wait_ge(s_fac, it * 4 + 2 * u + 1)
                    v4 = "p (h a b) -> p h a b"
                    e1 = e1_slot[u].rearrange(v4, h=HG, a=LA)
                    t2 = t2_tmp.rearrange(v4, h=HG, a=LA)
                    b1 = bcast(e_re[:, hs, L0 + LA:NSTEP], 2, LA)
                    b2 = bcast(e_im[:, hs, L0 + LA:NSTEP], 2, LA)
                    lc.mark(tt(t2, bcast(a2[:, hs, :], 3, LB), b2, ALU.mult))
                    lc.mark(tt(e1, bcast(a1[:, hs, :], 3, LB), b1, ALU.mult))
                    p1 = p1_slot[u].rearrange(v4, h=HG, a=BATCH)
                    p2 = p2_slot[u].rearrange(v4, h=HG, a=BATCH)
                    lc.mark(tt(p1, bcast(c_re[:, hs, :], 3, L0), bcast(g1[:, hs, :], 2, BATCH), ALU.mult))
                    dve.wait_ge(s_dve, it * 6 + (base + 3 * u + 2))
                    tt(e1_slot[u], e1_slot[u], t2_tmp, ALU.add).then_inc(s_fac, 1)
                    tt(p2, bcast(c_im[:, hs, :], 3, L0), bcast(g2[:, hs, :], 2, BATCH), ALU.mult)\
                        .then_inc(s_fac, 1)
                dve.wait_ge(s_whi, it + 5)
                w_low(w_lo[:, bass.ds(it, 1), :], w_stage[:, :].unsqueeze(1), w_hi[:, bass.ds(it, 1), :].bitcast(F32))
                assert lc.k == 6
            ch.k = base + 6 * (NGRP // 2)

            def rsqrt(c, y, var_in, var, i32, tmp):
                c.link(ts(var, var_in, EPS, None, ALU.add))
                c.link(ts(i32, var.bitcast(I32), 1, None, ALU.logical_shift_right))
                c.link(ts(y.bitcast(I32), i32, -1.0, RSQRT_MAGIC, ALU.mult, ALU.add))
                for _ in range(4):
                    c.link(tt(tmp, y, y, ALU.mult))
                    c.link(stt(tmp, tmp, -0.5, var, ALU.mult, ALU.mult))
                    c.link(stt(y, tmp, 1.5, y, ALU.add, ALU.mult))

            dve.wait_ge(s_const, N_CONST)
            ch.mark(v.tensor_reduce(in_place[:, :], ident[:, :].rearrange("p (a r) -> p r a", r=REP),
                                    AX.X, ALU.add))
            ch.link(v.tensor_reduce(in_group[:, :],
                                    ident[:, :].rearrange("p (q g r) -> p g q r", q=4, r=REP),
                                    AX.XY, ALU.add))
            ch.mark(v.tensor_copy(group_sel[:, :, :], bcast(in_group[:, :], 2, P)))
            base_b = ch.k
            PER_B = SB + 1 + 15
            with dve.Fori(0, BATCH // SB) as i:
                c = Chain(dve, s_dve, i * PER_B + base_b)
                for n in range(SB):
                    dve.wait_ge(s_xld[n], i * 16 + 16)
                    v.bn_stats(bst[:, n, 0:6], x_tok[n][:, 0:512])
                    c.mark(v.bn_stats(bst[:, n, 6:12], x_tok[n][:, 512:1024]))
                c.wait()
                carry_dve()
                for n in range(SB):
                    ins = v.bn_aggr(bmv[:, n, :], bst[:, n, :])
                c.link(ins)
                rsqrt(c, bvr[:, 1, :], bmv[:, :, 1], bvr[:, 0, :], bvr[:, 2, :].bitcast(I32), bvr[:, 3, :])
                for n in range(SB):
                    ts(x_tok[n][:, :], x_tok[n][:, :], bmv[:, n, 0:1], bvr[:, 1, n:n + 1],
                       ALU.subtract, ALU.mult).then_inc(s_xn, 1)
                for n in range(2 * SB):
                    b, half = n // 2, n % 2
                    dve.wait_ge(s_thi, i * (2 * SB) + n + 1)
                    part = (slice(None), slice(half * 4, half * 4 + 4), slice(b * P, (b + 1) * P))
                    tt(xt_lo[part], bank[TBANK[n % 4]][:, :].rearrange("p (k t) -> p k t", k=4),
                       xt_hi[part].bitcast(F32), ALU.subtract).then_inc(s_tlo, 1)
                assert c.k == PER_B, c.k
            ch.k = base_b + PER_B * (BATCH // SB)

            def maxima(b, slot, gg):
                for j in range(GJ):
                    dve.wait_ge(s_sq, b * 8 + gg * GJ + j + 1)
                    h0 = (gg * GJ + j) * REP
                    v.tensor_reduce(row_max[slot][:, 0, h0:h0 + REP],
                                    bank[2 + j % 2][:, :].rearrange("p (r k) -> p r k", r=REP),
                                    AX.X, ALU.max).then_inc(s_mx, 1)

            def shifts(b, slot):
                dve.wait_ge(s_mx, b * 8 + 8)
                v.tensor_copy(row_max[slot][:, 1:4, :], bcast(row_max[slot][:, 0, :], 1, 3))\
                    .then_inc(s_mc, 1)
                dve.wait_ge(s_mt, b + 1)
                stt(shift[slot][:, :, :], bcast(bank[4][:, 0:P], 1, REP), -1.0,
                    bcast(in_place[:, :], 2, P), ALU.mult, ALU.mult).then_inc(s_sh, 1)

            def normalise(c, b, slot, gg):
                dve.wait_ge(s_pv, b * 2 + gg + 1)
                after(dve, s_nrm, b * 2 + gg - 1)
                after(dve, s_olo, b * 2 + gg - 3)
                c.link(v.reciprocal(rsum[gg][:, :], bank[7][:, :]))
                tt(o_t[slot][:, gg * 512:(gg + 1) * 512], bank[6][:, :], rsum[gg][:, :], ALU.mult)\
                    .then_inc(s_nrm, 1)

            def context_lo(b, slot, gg):
                dve.wait_ge(s_ohi, b * 2 + gg + 1)
                cols = slice(gg * 512, (gg + 1) * 512)
                tt(o_lo[slot][:, cols], o_t[slot][:, cols], o_hi[slot][:, cols].bitcast(F32), ALU.subtract)\
                    .then_inc(s_olo, 1)

            def add_residual(b, slot):
                dve.wait_ge(s_xb, b + 1)
                after(dve, s_fin, b - 1)
                for n in range(2):
                    dve.wait_ge(s_y, b * 2 + n + 1)
                    cols = slice(n * 512, (n + 1) * 512)
                    ins = tt(h2[slot][:, cols], bank[n][:, :], x_res[slot][:, cols], ALU.add)
                ins.then_inc(s_h2, 1)

            def norm_rows(c, b, slot):
                dve.wait_ge(s_h2, b + 1)
                v.bn_stats(cst[:, 0:6], h2[slot][:, 0:512])
                c.link(v.bn_stats(cst[:, 6:12], h2[slot][:, 512:1024]))
                carry_dve()
                c.link(v.bn_aggr(cmv[:, :], cst[:, :]))
                rsqrt(c, rstd2[slot][:, :], cmv[:, 1:2], cvr[:, 0:1], cvr[:, 2:3].bitcast(I32), cvr[:, 3:4])
                after(dve, s_ht, b * 2)
                ts(hn[:, :], h2[slot][:, :], cmv[:, 0:1], rstd2[slot][:, :], ALU.subtract, ALU.mult)\
                    .then_inc(s_hn, 1)
                c.link(stt(nmr2[slot][:, :], cmv[:, 0:1], -1.0, rstd2[slot][:, :], ALU.mult, ALU.mult))

            def route(c, b, slot):
                dve.wait_ge(s_rt, b + 1)
                c.link(tt(logit[:, :], bank[3][:, 0:NE], rb_all[:, :], ALU.add))
                carry_dve()
                c.link(v.max(ranked[:, :], logit[:, :]))
                carry_dve()
                c.mark(v.match_replace(out=struck[:, :], in_to_replace=ranked[:, :], in_values=logit[:, :],
                                       imm_value=LOWEST))
                ts(neg_top[:, :], ranked[:, 0:1], -1.0, None, ALU.mult).then_inc(s_lg, 1)
                c.wait()
                c.link(tt(chosen[:, :], struck[:, :], logit[:, :], ALU.not_equal))
                dve.wait_ge(s_ex, b + 1)
                c.mark(v.reciprocal(rz[:, :], zsum[:, :]))
                c.link(stt(expd[:, :], expd[:, :], 1.0, chosen[:, :], ALU.mult, ALU.mult,
                           accum_out=wsum[:, :]))
                c.link(tt(wsum[:, :], wsum[:, :], rz[:, :], ALU.mult))
                after(dve, s_wt, b)
                ts(w_aug[:, 0:NE], expd[:, :], rz[:, :], None, ALU.mult)
                tt(w_aug[:, NE:NE + 1], nmr2[slot][:, :], wsum[:, :], ALU.mult)
                ts(hscale[slot][:, :], wsum[:, :], rstd2[slot][:, :], 1.0, ALU.mult, ALU.add)\
                    .then_inc(s_wa, 1)

            def finish(b, slot):
                dve.wait_ge(s_mix, b + 1)
                dve.wait_ge(s_out[slot], out_count(b))
                for n in range(2):
                    cols = slice(n * 512, (n + 1) * 512)
                    ins = stt(y_out[slot][:, cols], h2[slot][:, cols], hscale[slot][:, :],
                              bank[n][:, :], ALU.mult, ALU.add)
                ins.then_inc(s_fin, 1)

            pair_of = [None]

            def out_count(b):
                return 16 * (b // 2 + 1) if isinstance(b, int) else pair_of[0] * 16 + 16

            def step(c, b, slot):
                if has(b + 1):
                    maxima(b + 1, 1 - slot, 0)
                if isinstance(b, int) and b == -1:
                    for k in range(KD):
                        dve.wait_ge(s_whi, 12 + k + 1)
                        w_low(w_lo[:, k, :], y_out[k % 2][:, :], w_hi[:, k, :].bitcast(F32))
                    dve.wait_ge(s_tab, 64)
                if has(b - 2):
                    norm_rows(c, b - 2, slot)
                if has(b - 3):
                    finish(b - 3, 1 - slot)
                if has(b + 1):
                    maxima(b + 1, 1 - slot, 1)
                    shifts(b + 1, 1 - slot)
                if has(b - 1):
                    context_lo(b - 1, 1 - slot, 1)
                if has(b):
                    normalise(c, b, slot, 0)
                if has(b - 2):
                    route(c, b - 2, slot)
                if has(b):
                    context_lo(b, slot, 0)
                if has(b - 1):
                    add_residual(b - 1, 1 - slot)
                if has(b):
                    normalise(c, b, slot, 1)

            PER_C = 18 + 7 + 2
            for b in range(-1, STEADY):
                step(ch, b, b % 2)
            base_c = ch.k
            with dve.Fori(0, N_STEADY) as pr:
                lc = Chain(dve, s_dve, pr * (2 * PER_C) + base_c)
                for u in range(2):
                    pair_of[0] = pr + u // 2
                    step(lc, pr * 2 + (STEADY + u), (STEADY + u) % 2)
                assert lc.k == 2 * PER_C, lc.k
            ch.k = base_c + 2 * PER_C * N_STEADY
            for b in range(STEADY + 2 * N_STEADY, BATCH + 3):
                step(ch, b, b % 2)

        @block.tensor
        def _(pe):
            mm = nc.tensor.matmul
            pe.sem_inc(s_xmm, 3)
            pe.sem_inc(s_tp, 8)
            pe.sem_inc(s_pj, 1)
            with pe.Fori(0, NGRP // 2) as it:
                for u in range(2):
                    pe.wait_ge(s_fac, it * 4 + 2 * u + 4)
                    pe.wait_ge(s_xev, it * 4 + 2 * u + 1)
                    for h in range(HG):
                        dst = bank[2 * u + h // 4][:, (h % 4) * L1:(h % 4 + 1) * L1]
                        e1 = e1_slot[u][:, h * L1:(h + 1) * L1]
                        mm(dst, p1_slot[u][:, h * P:(h + 1) * P], e1, start=True, stop=False)
                        ins = mm(dst, p2_slot[u][:, h * P:(h + 1) * P], e1, start=False, stop=True)
                        if h % 4 == 3:
                            ins.then_inc(s_xmm, 1)

            def split_product(dst, parts):
                for n, (lh, ll, rh, rl) in enumerate(parts):
                    mm(dst, lh, rh, start=n == 0, stop=False)
                    mm(dst, lh, rl, start=False, stop=False)
                    ins = mm(dst, ll, rh, start=False, stop=n == len(parts) - 1)
                return ins

            def kv_cols(w, k, c0, n):
                return w[:, k // 2, (k % 2) * 512 + c0:(k % 2) * 512 + c0 + n]

            pe.wait_ge(s_const, N_CONST)
            with pe.Fori(0, BATCH // SB) as i:
                for n in range(2 * SB):
                    b, half = n // 2, n % 2
                    pe.wait_ge(s_tlo, i * (2 * SB) + n + 1)
                    if half == 0:
                        pe.wait_ge(s_xn, i * SB + b + 1)
                    for k in range(4):
                        c = (half * 4 + k) * P
                        ins = nc.tensor.transpose(bank[TBANK[n % 4]][:, k * P:(k + 1) * P],
                                                  x_tok[b][:, c:c + P], ident[:, :])
                    ins.then_inc(s_tp, 1)
                pe.wait_ge(s_tlo, i * (2 * SB) + 2 * SB + 4)
                for t in range(14):
                    dst = bank[2 + t % 4]
                    if t >= 4:
                        pe.wait_ge(s_pja, i * 14 + t - 3)
                    if t < GG:
                        ins = split_product(dst[:, :], [
                            (kv_cols(kv_hi, k, t * P, P), kv_cols(kv_lo, k, t * P, P), xt_hi[:, k, :],
                             xt_lo[:, k, :]) for k in range(KD)])
                    elif t < 10:
                        cols = slice((t - GG) * P, (t - GG + 1) * P)
                        ins = split_product(dst[:, :], [
                            (w_hi[:, k, cols], w_lo[:, k, cols], xt_hi[:, k, :], xt_lo[:, k, :])
                            for k in range(KD)])
                    else:
                        tok = slice((t - 10) * P, (t - 9) * P)
                        ins = split_product(dst[:, 0:NG * HD], [
                            (xt_hi[:, k, tok], xt_lo[:, k, tok], kv_cols(kv_hi, k, 256, 256),
                             kv_cols(kv_lo, k, 256, 256)) for k in range(KD)])
                    ins.then_inc(s_pj, 1)

            def row_scores(b, slot, gg):
                if gg == 0:
                    pe.wait_ge(s_cast, b + 1)
                for j in range(GJ):
                    rows = slice(j * HD, (j + 1) * HD)
                    after(pe, s_mx, b * 8 + gg * GJ + j - 1)
                    if gg == 0 and j == 1 and has(b - 4):
                        pe.wait_ge(s_lg, b - 3)
                    dst = bank[2 + j % 2]
                    mm(dst[:, :], ident_bf[:, :], above_bf[:, :, :].rearrange("p r k -> p (r k)"),
                       start=True, stop=False, skip_group_check=True)
                    for r in range(REP):
                        ins = mm(dst[:, r * P:(r + 1) * P], q_bf[slot][rows, gg * REP + r, :],
                                 k_bf[slot][rows, gg, :], start=False, stop=r == REP - 1,
                                 skip_group_check=True)
                    ins.then_inc(s_sq, 1)

            def transpose_max(b, slot, fresh):
                pe.wait_ge(s_mc, b + 1)
                if not fresh:
                    pe.wait_ge(s_pe, b * 8 - 4)
                nc.tensor.transpose(bank[4][:, 0:P], row_max[slot][:, :, :].rearrange("p q h -> p (q h)"),
                                    ident[:, :]).then_inc(s_mt, 1)

            def key_scores(b, slot, gg):
                if gg == 0:
                    pe.wait_ge(s_sh, b + 1)
                    after(pe, s_wte, b - 2)
                elif has(b + 1):
                    pe.wait_ge(s_sh, b + 2)
                for j in range(GJ):
                    rows = slice(j * HD, (j + 1) * HD)
                    after(pe, s_pe, b * 8 + gg * GJ + j - 1)
                    dst = bank[4 + j % 2][:, :].rearrange("p (r q) -> p r q", r=REP)
                    mm(dst, k_t[slot][rows, gg, :], q_t[slot][rows, gg * REP:(gg + 1) * REP, :],
                       start=True, stop=False)
                    mm(dst, group_sel[rows, gg * GJ + j, :], shift[slot][rows, :, :],
                       start=False, stop=True).then_inc(s_sk, 1)

            def values(b, slot, gg):
                pe.wait_ge(s_msk, b * 2 + gg + 2)
                after(pe, s_nrm, b * 2 + gg)
                for j in range(GJ):
                    mm(bank[6][j * HD:(j + 1) * HD, :], v_tok[slot][:, gg * GJ + j, :], p_t[gg][:, j, :],
                       start=True, stop=True)
                for j in range(GJ):
                    ins = mm(bank[7][j * HD:(j + 1) * HD, :], ones32[:, :], p_t[gg][:, j, :],
                             start=True, stop=True)
                ins.then_inc(s_pv, 1)

            def project(b, slot, n):
                if n == 0:
                    pe.wait_ge(s_olo, b * 2 + 2)
                    after(pe, s_fin, b - 1)
                cols = slice(n * 512, (n + 1) * 512)
                split_product(bank[n][:, :], [
                    (o_hi[slot][:, k * P:(k + 1) * P], o_lo[slot][:, k * P:(k + 1) * P], w_hi[:, k, cols],
                     w_lo[:, k, cols]) for k in range(KD)]).then_inc(s_y, 1)

            def transpose_rows(b):
                pe.wait_ge(s_hn, b + 1)
                for half in range(2):
                    for k in range(4):
                        c = (half * 4 + k) * P
                        ins = nc.tensor.transpose(bank[2 + half][:, k * P:(k + 1) * P], hn[:, c:c + P],
                                                  ident[:, :])
                    ins.then_inc(s_ht, 1)

            def router(b):
                pe.wait_ge(s_hte, b * 2 + 2)
                for k in range(KD):
                    ins = mm(bank[3][:, 0:NE], hn_t[:, k, :], rw[:, k, :], start=k == 0, stop=k == KD - 1)
                ins.then_inc(s_rt, 1)

            def transpose_weights(b):
                pe.wait_ge(s_wa, b + 1)
                nc.tensor.transpose(bank[4][0:NE + 1, 0:P], w_aug[:, :], ident[:, :]).then_inc(s_wt, 1)

            def mix(b):
                pe.wait_ge(s_wte, b + 1)
                pe.wait_ge(s_h2, b + 2 if not isinstance(b, int) else min(b + 2, BATCH))
                for n in range(2):
                    ins = mm(bank[n][:, :], w_aug_t[:, :], eb_one[:, n * 512:(n + 1) * 512],
                             start=True, stop=True)
                ins.then_inc(s_mix, 1)

            def step(b, slot):
                if has(b + 1):
                    row_scores(b + 1, 1 - slot, 0)
                if has(b - 3):
                    transpose_weights(b - 3)
                if has(b):
                    key_scores(b, slot, 0)
                if has(b - 3):
                    mix(b - 3)
                if has(b + 1):
                    row_scores(b + 1, 1 - slot, 1)
                    transpose_max(b + 1, 1 - slot, isinstance(b, int) and b < 0)
                if has(b):
                    values(b, slot, 0)
                if has(b - 1):
                    if isinstance(b, int) and b == 1:
                        pe.wait_ge(s_whi, 12 + KD)
                        pe.wait_ge(s_wlo, 12 + KD)
                        pe.wait_ge(s_tab, 64)
                        pe.wait_ge(s_ones, 1)
                    project(b - 1, 1 - slot, 0)
                if has(b - 2):
                    transpose_rows(b - 2)
                if has(b):
                    key_scores(b, slot, 1)
                if has(b - 2):
                    router(b - 2)
                if has(b - 1):
                    project(b - 1, 1 - slot, 1)
                if has(b):
                    values(b, slot, 1)

            pe.wait_ge(s_pja, 14 * (BATCH // SB))
            steps_of_c(pe, step)


def kernel(x, L0_tok_log_dt, L0_tok_B, L0_tok_inv_A_real, L0_tok_A_imag, L0_attn_Wq, L0_attn_Wkv,
           L0_attn_Wo, L0_attn_bo, L0_ffn_router_weight, L0_ffn_router_bias, L0_ffn_expert_bias):
    import concourse.bacc as bacc
    from concourse.bass_utils import run_bass_kernel_spmd

    wq = np.asarray(L0_attn_Wq).reshape(D, GG, GJ, REP, HD).transpose(0, 1, 3, 2, 4).reshape(KD, P, D)
    wkv = np.asarray(L0_attn_Wkv).reshape(D, NG, 2, HD).transpose(0, 2, 1, 3).reshape(4, 2, P, 512)
    wkv = wkv.transpose(0, 2, 1, 3).reshape(4, P, D)
    wo = np.asarray(L0_attn_Wo).reshape(GG, GJ, REP, HD, D).transpose(0, 2, 1, 3, 4).reshape(KD, P, D)
    arrays = {
        "c_re_im": np.asarray(x).transpose(3, 2, 1, 0),
        "log_dt": np.asarray(L0_tok_log_dt),
        "b_re_im": np.asarray(L0_tok_B).transpose(2, 1, 0),
        "inv_a": np.asarray(L0_tok_inv_A_real).T,
        "a_imag": np.asarray(L0_tok_A_imag).T,
        "w_qkv": np.concatenate([wq, wkv]),
        "w_out": wo,
        "bo": np.asarray(L0_attn_bo),
        "router_t": np.asarray(L0_ffn_router_weight).T,
        "rbias": np.asarray(L0_ffn_router_bias),
        "ebias": np.asarray(L0_ffn_expert_bias),
    }
    arrays = {n: np.ascontiguousarray(a) for n, a in arrays.items()}
    nc = bacc.Bacc("TRN2", target_bir_lowering=False, num_devices=1)
    args = [nc.dram_tensor(n, a.shape, mybir.dt.from_np(a.dtype), kind="ExternalInput").ap()
            for n, a in arrays.items()]
    out = nc.dram_tensor("out", (BATCH, T, D), F32, kind="ExternalOutput").ap()
    build(nc, *args, out)
    r = run_bass_kernel_spmd(nc, [arrays], core_ids=[0])
    return r.results[0]["out"]
```

```python
import numpy as np
import concourse.bass as bass
from concourse import mybir
from contextlib import ExitStack

F32 = mybir.dt.float32
F32R = mybir.dt.float32r
BF16 = mybir.dt.bfloat16
I32 = mybir.dt.int32
ALU = mybir.AluOpType
ACT = mybir.ActivationFunctionType
AX = mybir.AxisListType

P = 128
BATCH, T, D = 16, 128, 1024
MODES = 64
L0, L1 = 8, 128
LA, LB = 8, 16
NSTEP = L0 + LA + LB
J_ONE = L0 + LA + 1
KD = D // P
NH, NG, HD = 32, 8, 32
REP = NH // NG
GG = 2
GJ = NG // GG
ROWS = 3 * HD
SB = 4
NE, TOPK = 64, 8
EPS = 1e-5
SCALE = 1.0 / HD ** 0.5
NEG = -1e30
LOWEST = -3e38

HG = 8
NGRP = T // HG
TWO_PI = 2.0 * np.pi
C1 = 6.28125
C2 = float(np.float32(round((TWO_PI - C1) * 2 ** 20) / 2 ** 20))
C3 = float(np.float32(TWO_PI - C1 - C2))
PI_IN = 3.1415925
ROUND = 1.5 * 2.0 ** 23
RSQRT_MAGIC = float(0x5F3759DF)


def bcast(ap, axis, n):
    a = ap.unsqueeze(axis)
    shape = list(a.shape)
    shape[axis] = n
    return a.broadcast_to(shape)


class Chain:

    def __init__(self, eng, sem, base=0):
        self.eng, self.sem, self.base, self.k = eng, sem, base, 0

    def mark(self, ins):
        ins.then_inc(self.sem, 1)
        self.k += 1

    def wait(self):
        self.eng.wait_ge(self.sem, self.base + self.k)

    def link(self, ins):
        self.mark(ins)
        self.wait()


def build(nc, c_re_im, log_dt, b_re_im, inv_a, a_imag, w_qkv, w_out, bo, router_t, rbias, ebias, out):
    x_scr = nc.dram_tensor("x_scratch", (BATCH * L0, T, L1), F32, kind="Internal").ap()
    q_scr = [nc.dram_tensor(f"q_scratch{n}", (BATCH, P, GG * REP, P), F32, kind="Internal").ap()
             for n in range(2)]
    k_scr = [nc.dram_tensor(f"k_scratch{n}", (NG, GJ * HD, BATCH // SB, P), F32, kind="Internal").ap()
             for n in range(2)]
    qb_scr = nc.dram_tensor("qb_scratch", (BATCH, P, GG * REP, P), BF16, kind="Internal").ap()
    kb_scr = nc.dram_tensor("kb_scratch", (NG, GJ * HD, BATCH // SB, P), BF16, kind="Internal").ap()

    es = ExitStack()
    with es:
        def sb(name, shape, dt=F32, stack=es):
            return stack.enter_context(nc.sbuf_tensor(name, shape, dt))

        def sem(name):
            return es.enter_context(nc.semaphore(name))

        w_hi = sb("w_hi", [P, KD, D], F32R)
        w_lo = sb("w_lo", [P, KD, D], F32R)
        ident = sb("ident", [P, P])
        ident_bf = sb("ident_bf", [P, P], BF16)
        above_bf = sb("above_bf", [P, REP, P], BF16)
        ones32 = sb("ones32", [P, HD])
        steps = sb("steps", [P, NSTEP])
        steps_i = sb("steps_i", [P, NSTEP], I32)
        half_pi = sb("half_pi", [P, 1])
        carrier = sb("carrier", [P, 2])
        in_group = sb("in_group", [P, NG])
        in_place = sb("in_place", [P, REP])
        group_sel = sb("group_sel", [P, NG, P], F32R)

        eab = ExitStack()
        kv_hi = sb("kv_hi", [P, KD // 2, D], F32R, stack=eab)
        kv_lo = sb("kv_lo", [P, KD // 2, D], F32R, stack=eab)

        ea = ExitStack()
        w_stage = sb("w_stage", [P, D], stack=ea)
        e_re = sb("e_re", [P, T, NSTEP], stack=ea)
        e_im = sb("e_im", [P, T, NSTEP], stack=ea)
        a1 = sb("a1", [P, T, LA], stack=ea)
        a2 = sb("a2", [P, T, LA], stack=ea)
        g1 = sb("g1", [P, T, L0], stack=ea)
        g2 = sb("g2", [P, T, L0], stack=ea)
        c_re = sb("c_re", [P, T, BATCH], stack=ea)
        c_im = sb("c_im", [P, T, BATCH], stack=ea)
        work = sb("work", [P, 9, D], stack=ea)
        th = work[:, 0:4, :].rearrange("p a (b j) -> p (a b) j", j=NSTEP)
        kk = work[:, 4:8, :].rearrange("p a (b j) -> p (a b) j", j=NSTEP)
        e1_slot = [work[:, 0, :], work[:, 1, :]]
        p1_slot = [work[:, 2, :], work[:, 3, :]]
        p2_slot = [work[:, 4, :], work[:, 5, :]]
        t2_tmp = work[:, 6, :]
        x_stage = [work[:, 7, :], work[:, 8, :]]
        names = ["ldt", "inva", "aim", "bre", "bim", "dt", "em", "ar", "ai", "sh", "tnh", "q2", "xr",
                 "den", "ni", "nr", "yr", "yi", "fr", "fi", "nfr", "m"]
        room = [t.rearrange("p (n t) -> p n t", t=T) for t in
                (work[:, 8, :], g1[:, :, :].rearrange("p t l -> p (t l)"),
                 g2[:, :, :].rearrange("p t l -> p (t l)"))]
        sm = {n: room[k // L0][:, k % L0, :] for k, n in enumerate(names)}
        ea.close()

        eb = ExitStack()
        v_all = sb("v_all", [P, BATCH, NG * HD], stack=eb)
        x_tok = [sb(f"x_tok{n}", [P, D], stack=eb) for n in range(SB)]
        xt_hi = sb("xt_hi", [P, KD, SB * P], F32R, stack=eb)
        xt_lo = sb("xt_lo", [P, KD, SB * P], F32R, stack=eb)
        hi_stage = [sb(f"hi_stage{n}", [P, SB * P], F32R, stack=eb) for n in range(4)]
        lo_stage = [sb(f"lo_stage{n}", [P, SB * P], stack=eb) for n in range(4)]
        bf_stage = [sb(f"bf_stage{n}", [P, SB * P], BF16, stack=eb) for n in range(4)]
        bst = sb("bst", [P, SB, 12], stack=eb)
        bmv = sb("bmv", [P, SB, 2], stack=eb)
        bvr = sb("bvr", [P, 4, SB], stack=eb)
        eb.close()
        eab.close()

        ec = ExitStack()
        p_t = [sb(f"p_t{n}", [P, GJ, REP * P], stack=ec) for n in range(2)]
        o_hi = [sb(f"o_hi{n}", [P, D], F32R, stack=ec) for n in range(2)]
        o_lo = [sb(f"o_lo{n}", [P, D], F32R, stack=ec) for n in range(2)]
        sb("v_all_place", [P, BATCH, NG * HD], stack=ec)
        q_bf = [sb(f"q_bf{n}", [P, GG * REP, P], BF16, stack=ec) for n in range(2)]
        k_bf = [sb(f"k_bf{n}", [P, GG, P], BF16, stack=ec) for n in range(2)]
        q_load, k_load = [], []
        for n in range(GG):
            q_load.append(sb(f"q_load{n}", [ROWS, GJ, REP * P], stack=ec))
            k_load.append(sb(f"k_load{n}", [ROWS, GJ, P], stack=ec))
        q_r = [sb(f"q_r{n}", [ROWS, REP * P], F32R, stack=ec) for n in range(2)]
        k_r = [sb(f"k_r{n}", [ROWS, GJ, P], F32R, stack=ec) for n in range(GG)]
        v_tok = [sb(f"v_tok{n}", [P, NG, HD], stack=ec) for n in range(2)]
        o_t = [sb(f"o_t{n}", [P, REP * P], stack=ec) for n in range(2)]
        rinv = sb("rinv", [P, REP * P], stack=ec)
        shift = sb("shift", [P, REP, P], F32R, stack=ec)
        row_max = [sb(f"row_max{n}", [P, 4, NH], stack=ec) for n in range(2)]
        x_res = [sb(f"x_res{n}", [P, D], stack=ec) for n in range(2)]
        h2 = [sb(f"h2_{n}", [P, D], stack=ec) for n in range(2)]
        hn = sb("hn", [P, D], stack=ec)
        hn_t = sb("hn_t", [P, KD, P], stack=ec)
        y_out = [sb(f"y_out{n}", [P, D], stack=ec) for n in range(2)]
        rw = sb("rw", [P, KD, NE], stack=ec)
        rb_all = sb("rb_all", [P, NE], stack=ec)
        eb_one = sb("eb_one", [NE + 1, D], stack=ec)
        bo_all = sb("bo_all", [P, D], stack=ec)
        cst = sb("cst", [P, 12], stack=ec)
        cmv = sb("cmv", [P, 2], stack=ec)
        cvr = sb("cvr", [P, 4], stack=ec)
        rstd2 = [sb(f"rstd2_{n}", [P, 1], stack=ec) for n in range(2)]
        nmr2 = [sb(f"nmr2_{n}", [P, 1], stack=ec) for n in range(2)]
        logit = sb("logit", [P, NE], stack=ec)
        ranked = sb("ranked", [P, TOPK], stack=ec)
        struck = sb("struck", [P, NE], stack=ec)
        neg_top = sb("neg_top", [P, 1], stack=ec)
        expd = sb("expd", [P, NE], stack=ec)
        zsum = sb("zsum", [P, 1], stack=ec)
        chosen = sb("chosen", [P, NE], stack=ec)
        wsum = sb("wsum", [P, 1], stack=ec)
        rz = sb("rz", [P, 1], stack=ec)
        w_aug = sb("w_aug", [P, NE + 1], stack=ec)
        w_aug_t = sb("w_aug_t", [NE + 1, P], stack=ec)
        hscale = [sb(f"hscale{n}", [P, 1], stack=ec) for n in range(2)]
        ec.close()

        bank = [es.enter_context(nc.psum_tensor(f"bank{n}", [P, 512], F32)) for n in range(8)]

        s_par = sem("s_par")
        s_c = sem("s_c")
        s_const = sem("s_const")
        s_steps = sem("s_steps")
        s_dt = sem("s_dt")
        s_angle = sem("s_angle")
        s_trig = sem("s_trig")
        s_decay = sem("s_decay")
        s_mag = sem("s_mag")
        s_etab = sem("s_etab")
        s_atab = sem("s_atab")
        s_wload = sem("s_wload")
        s_whi = sem("s_whi")
        s_wlo = sem("s_wlo")
        s_fac = sem("s_fac")
        s_xmm = sem("s_xmm")
        s_xev = sem("s_xev")
        s_xst = [sem(f"s_xst{n}") for n in range(2)]
        s_dve = sem("s_dve")
        s_xld = [sem(f"s_xld{n}") for n in range(SB)]
        s_xn = sem("s_xn")
        s_tp = sem("s_tp")
        s_thi = sem("s_thi")
        s_tlo = sem("s_tlo")
        s_pj = sem("s_pj")
        s_pja = sem("s_pja")
        s_pjl = sem("s_pjl")
        s_qst = [sem(f"s_qst{n}") for n in range(4)]
        s_tab = sem("s_tab")
        s_wol = [sem(f"s_wol{n}") for n in range(2)]
        s_qk = [sem(f"s_qk{n}") for n in range(GG)]
        s_qc = sem("s_qc")
        s_kc = sem("s_kc")
        s_rld = [sem(f"s_rld{n}") for n in range(2)]
        s_qb = [sem(f"s_qb{n}") for n in range(2)]
        s_vt = sem("s_vt")
        s_sq = sem("s_sq")
        s_mx = sem("s_mx")
        s_mc = sem("s_mc")
        s_mt = sem("s_mt")
        s_sh = sem("s_sh")
        s_sk = sem("s_sk")
        s_pe = sem("s_pe")
        s_msk = sem("s_msk")
        s_pv = sem("s_pv")
        s_nrm = sem("s_nrm")
        s_ohi = sem("s_ohi")
        s_olo = sem("s_olo")
        s_xb = sem("s_xb")
        s_y = sem("s_y")
        s_r0 = sem("s_r0")
        s_h2 = sem("s_h2")
        s_nmr = sem("s_nmr")
        s_hn = sem("s_hn")
        s_ht = sem("s_ht")
        s_hte = sem("s_hte")
        s_rt = sem("s_rt")
        s_lg = sem("s_lg")
        s_ex = sem("s_ex")
        s_wa = sem("s_wa")
        s_wt = sem("s_wt")
        s_wte = sem("s_wte")
        s_mix = sem("s_mix")
        s_fin = sem("s_fin")
        s_out = [sem(f"s_out{n}") for n in range(2)]
        s_ones = sem("s_ones")

        s_carry = sem("s_carry")
        s_kst = sem("s_kst")
        SLOT_STORES = [sum(1 if t < GG else 3 for t in range(10) if t % 4 == n) for n in range(4)]
        K_STORES = 3 * GJ - 1
        QK = GG + GG * REP
        TBANK = [0, 1, 6, 7]
        N_CONST = 8

        def after(eng, semaphore, count):
            if not (isinstance(count, int) and count <= 0):
                eng.wait_ge(semaphore, count)

        STEADY = 3
        N_STEADY = (BATCH - 1 - STEADY) // 2

        def has(b):
            return not isinstance(b, int) or 0 <= b < BATCH

        def carry_dve():
            nc.vector.tensor_copy(carrier[:, 0:1], ones32[:, 0:1])

        def carry_pool():
            nc.gpsimd.tensor_tensor(carrier[:, 1:2], ones32[:, 0:1], ones32[:, 0:1], ALU.mult)

        block = es.enter_context(nc.Block())

        @block.sync
        def _(sp):
            sp.dma_start(sm["ldt"][:, :], log_dt.rearrange("(a h) -> a h", a=1).broadcast_to([P, T]))\
              .then_inc(s_par, 16)
            for half in (0, MODES):
                rows = slice(half, half + MODES)
                sp.dma_start(sm["inva"][rows, :], inv_a).then_inc(s_par, 16)
                sp.dma_start(sm["aim"][rows, :], a_imag).then_inc(s_par, 16)
                sp.dma_start(sm["bre"][rows, :], b_re_im[0]).then_inc(s_par, 16)
                sp.dma_start(sm["bim"][rows, :], b_re_im[1]).then_inc(s_par, 16)
            for k in range(8, 12):
                if k > 8:
                    sp.wait_ge(s_whi, k - 8)
                    sp.wait_ge(s_wlo, k - 8)
                sp.dma_start(w_stage[:, :], w_qkv[k]).then_inc(s_wload, 16)
                if k == 8:
                    for half in (0, MODES):
                        rows = slice(half, half + MODES)
                        sp.dma_start(c_re[rows, :, :], c_re_im[0]).then_inc(s_c, 16)
                        sp.dma_start(c_im[rows, :, :], c_re_im[1]).then_inc(s_c, 16)
            for u in range(2):
                sp.sem_inc(s_xst[u], 16)
                sp.sem_inc(s_out[u], 16)
            with sp.Fori(0, NGRP // 2) as it:
                sp.wait_ge(s_whi, it + 4)
                sp.wait_ge(s_wlo, it + 4)
                sp.dma_start(w_stage[:, :], w_qkv[it]).then_inc(s_wload, 16)
                for u in range(2):
                    sp.wait_ge(s_xev, it * 4 + 2 * u + 5)
                    sp.dma_start(x_scr[:, bass.ds(it * (2 * HG) + u * HG, HG), :],
                                 x_stage[u].rearrange("p (h l) -> p h l", h=HG)).then_inc(s_xst[u], 16)
            for n in range(4):
                sp.sem_inc(s_qst[n], 16)
            with sp.Fori(0, BATCH // SB) as i:
                for t in range(GG + GG * REP):
                    sp.wait_ge(s_pjl, i * QK + t + 1)
                    for stage, ks, qs in ((hi_stage, k_scr[0], q_scr[0]), (lo_stage, k_scr[1], q_scr[1]),
                                          (bf_stage, kb_scr, qb_scr)):
                        src = stage[t % 4][:, :].rearrange("p (s t) -> p s t", s=SB)
                        if stage is hi_stage:
                            src = src.bitcast(F32)
                        if t < GG:
                            for g in range(GJ):
                                last = g == GJ - 1 and stage is bf_stage
                                sp.dma_start(ks[t * GJ + g].rearrange("(j w) i k -> w j i k", j=GJ)
                                             [:, :, bass.ds(i, 1), :],
                                             src[g * HD:(g + 1) * HD, :, :].unsqueeze(2))\
                                  .then_inc(s_qst[t % 4] if last else s_kst, 16)
                        else:
                            sp.dma_start(qs[bass.ds(i * SB, SB), :, t - GG, :].rearrange("s p t -> p s t"),
                                         src).then_inc(s_qst[t % 4], 16)
            for n in range(4):
                sp.wait_ge(s_qst[n], 16 * (1 + SLOT_STORES[n] * (BATCH // SB)))
            sp.wait_ge(s_kst, 16 * K_STORES * GG * (BATCH // SB))

            def load_bf(b, slot, group):
                after(sp, s_sq, b * 8 - 8)
                sp.dma_start(q_bf[slot][:, :, :], qb_scr[b]).then_inc(s_qb[slot], 16)
                sp.dma_start(k_bf[slot][:, :, :], kb_scr[group][:, slot * GG:(slot + 1) * GG, :])\
                  .then_inc(s_qb[slot], 16)

            def load_unit(b, slot, gg, group):
                if not (isinstance(b, int) and b < 1):
                    sp.wait_ge(s_qc, b * 8 - 4 + gg * GJ)
                    sp.sem_inc(s_carry, 1)
                for n, (query_part, key_part) in enumerate(((0, 0), (1, 0), (0, 1))):
                    rows = slice(n * HD, (n + 1) * HD)
                    sp.dma_start(q_load[gg][rows, :, :],
                                 q_scr[query_part][b].rearrange("(j w) (g r) q -> w j g (r q)", j=GJ, g=GG)
                                 [:, :, gg, :]).then_inc(s_qk[gg], 16)
                    sp.dma_start(k_load[gg][rows, :, :],
                                 k_scr[key_part][group].rearrange("(j w) i k -> w j i k", j=GJ)
                                 [:, :, slot * GG + gg, :]).then_inc(s_qk[gg], 16)

            x_rows = x_scr.rearrange("(b m) t l -> b t m l", b=BATCH)

            def load_res(b, slot):
                after(sp, s_h2, b - 1)
                sp.dma_start(x_res[slot][:, :].rearrange("p (m l) -> p m l", m=L0), x_rows[b])\
                  .then_inc(s_rld[slot], 16)

            for b in range(2):
                load_bf(b, b, 0)
            load_unit(0, 0, 0, 0)
            sp.wait_ge(s_pja, 14 * (BATCH // SB))
            load_unit(0, 0, 1, 0)
            for k in range(KD):
                if k >= 2:
                    sp.wait_ge(s_whi, 12 + k - 1)
                    sp.wait_ge(s_wlo, 12 + k - 1)
                sp.dma_start(y_out[k % 2][:, :], w_out[k]).then_inc(s_wol[k % 2], 16)
            sp.dma_start(bo_all[:, :], bo.rearrange("(a e) -> a e", a=1).broadcast_to([P, D]))\
              .then_inc(s_tab, 16)
            sp.dma_start(rw[:, :, :], router_t.rearrange("(k p) e -> p k e", p=P)).then_inc(s_tab, 16)
            sp.dma_start(rb_all[:, :], rbias.rearrange("(a e) -> a e", a=1).broadcast_to([P, NE]))\
              .then_inc(s_tab, 16)
            sp.dma_start(eb_one[0:NE, :], ebias).then_inc(s_tab, 16)

            def step(b, slot, groups=None):
                next_group, group = groups or ((b + 1) // 2, (b + 2) // 2)
                if not isinstance(b, int) or 0 <= b < BATCH - 2:
                    load_bf(b + 2, slot, group)
                if has(b):
                    load_res(b, slot)
                if has(b) and has(b + 1):
                    load_unit(b + 1, 1 - slot, 0, next_group)
                if has(b - 3):
                    sp.wait_ge(s_fin, b - 2)
                    sp.dma_start(out[b - 3], y_out[1 - slot][:, :]).then_inc(s_out[1 - slot], 16)
                if has(b) and has(b + 1):
                    load_unit(b + 1, 1 - slot, 1, next_group)

            for b in range(-1, STEADY):
                step(b, b % 2)
            with sp.Fori(0, N_STEADY - 1) as pr:
                for u in range(2):
                    step(pr * 2 + (STEADY + u), (STEADY + u) % 2,
                         (pr + (STEADY + u + 1) // 2, pr + (STEADY + u + 2) // 2))
            for b in range(STEADY + 2 * (N_STEADY - 1), BATCH + 3):
                step(b, b % 2)
            for u in range(2):
                sp.wait_ge(s_out[u], 16 * (BATCH // 2 + 1))

        @block.gpsimd
        def _(pool):
            g = nc.gpsimd
            g.iota(steps_i[:, 0:L0], pattern=[[P, L0]], base=0, channel_multiplier=0).then_inc(s_steps, 1)
            g.iota(steps_i[:, L0:L0 + LA], pattern=[[LB, LA]], base=0, channel_multiplier=0).then_inc(s_steps, 1)
            g.iota(steps_i[:, L0 + LA:NSTEP], pattern=[[1, LB]], base=0, channel_multiplier=0)\
             .then_inc(s_steps, 1)
            g.memset(half_pi[:, :], float(np.pi / 2)).then_inc(s_const, 1)
            g.memset(ident[:, :], 0.0).then_inc(s_const, 1)
            g.memset(ident_bf[:, :], 0.0).then_inc(s_const, 1)
            g.memset(above_bf[:, :, :], 0.0).then_inc(s_const, 1)
            g.memset(ones32[:, :], 1.0).then_inc(s_const, 1)
            pool.wait_ge(s_const, 5)
            for m in (ident, ident_bf):
                g.affine_select(out=m[:, :], in_=m[:, :], compare_op=ALU.not_equal, fill=1.0, base=0,
                                pattern=[[-1, P]], channel_multiplier=1).then_inc(s_const, 1)
            g.affine_select(out=above_bf[:, :, :], in_=above_bf[:, :, :], compare_op=ALU.is_ge, fill=NEG,
                            base=0, pattern=[[0, REP], [-1, P]], channel_multiplier=1).then_inc(s_const, 1)
            for u in range(2):
                pool.wait_ge(s_xst[u], 16 * (NGRP // 2 + 1))
            x_rows = x_scr.rearrange("(b m) t l -> b t m l", b=BATCH)
            with pool.Fori(0, BATCH // SB) as i:
                for b in range(SB):
                    pool.wait_ge(s_tp, i * (2 * SB) + 2 * b + 2)
                    pool.dma_start(x_tok[b][:, :].rearrange("p (m l) -> p m l", m=L0), x_rows[i * SB + b])\
                        .then_inc(s_xld[b], 16)
            pool.sem_inc(s_msk, 1)
            for n in range(4):
                pool.wait_ge(s_qst[n], 16 * (1 + SLOT_STORES[n] * (BATCH // SB)))
            pool.wait_ge(s_pja, 14 * (BATCH // SB))
            g.memset(eb_one[NE:NE + 1, :], 1.0).then_inc(s_ones, 1)
            pool.wait_ge(s_ones, 1)
            pool.wait_ge(s_tab, 64)
            def mask(b, gg):
                pool.wait_ge(s_pe, b * 8 + GJ * (gg + 1))
                pool.wait_ge(s_msk, b * 2 + gg + 1)
                carry_pool()
                view = p_t[gg][:, :, :].rearrange("p j (r q) -> p (j r) q", r=REP)
                g.affine_select(out=view, in_=view, compare_op=ALU.is_ge, fill=0.0, base=0,
                                pattern=[[0, GJ * REP], [1, P]], channel_multiplier=-1)\
                 .then_inc(s_msk, 1)

            def context_lo(b, slot, gg):
                pool.wait_ge(s_ohi, b * 2 + gg + 1)
                cols = slice(gg * 512, (gg + 1) * 512)
                g.tensor_tensor(o_lo[slot][:, cols], o_t[gg][:, :], o_hi[slot][:, cols].bitcast(F32),
                                ALU.subtract).then_inc(s_olo, 1)

            def step(b, slot):
                if has(b):
                    mask(b, 0)
                if has(b - 1):
                    context_lo(b - 1, 1 - slot, 1)
                if has(b):
                    mask(b, 1)
                    context_lo(b, slot, 0)
                    pool.wait_ge(s_rld[slot], loaded(b))
                    g.tensor_tensor(x_res[slot][:, :], x_res[slot][:, :], bo_all[:, :], ALU.add)\
                     .then_inc(s_xb, 1)

            pair_of_pool = [None]

            def loaded(b):
                return 16 * (b // 2 + 1) if isinstance(b, int) else pair_of_pool[0] * 16 + 16

            step(0, 0)
            with pool.Fori(0, (BATCH - 2) // 2) as pr:
                for u in range(2):
                    pair_of_pool[0] = pr + u
                    step(pr * 2 + (u + 1), 1 - u)
            for b in range(BATCH - 1, BATCH + 1):
                step(b, b % 2)

        @block.scalar
        def _(act):
            a = nc.scalar
            act.sem_inc(s_xev, 3)
            act.wait_ge(s_par, 9 * 16)
            a.activation(sm["dt"][:, :], sm["ldt"][:, :], ACT.Exp).then_inc(s_dt, 1)
            a.activation(sm["em"][:, :], sm["inva"][:, :], ACT.Exp).then_inc(s_dt, 1)

            for k in range(KD // 2):
                act.wait_ge(s_wload, 16 * (k + 1))
                a.activation(kv_hi[:, k, :], w_stage[:, :], ACT.Copy).then_inc(s_whi, 1)
            act.wait_ge(s_angle, 1)
            a.activation(e_im[:, :, :], th, ACT.Sin).then_inc(s_trig, 1)
            a.activation(sm["sh"][:, :], th[:, :, J_ONE], ACT.Sin, scale=0.5).then_inc(s_trig, 1)
            act.wait_ge(s_angle, 2)
            act.wait_ge(s_const, 1)
            a.activation(e_re[:, :, :], kk, ACT.Sin, bias=half_pi[:, 0:1]).then_inc(s_trig, 1)
            act.wait_ge(s_trig, 3)
            act.wait_ge(s_decay, 1)
            a.activation(kk, th, ACT.Exp).then_inc(s_mag, 1)
            a.activation(sm["tnh"][:, :], sm["ar"][:, :], ACT.Tanh, scale=0.5).then_inc(s_mag, 1)
            act.wait_ge(s_etab, 1)
            top, bot = slice(0, MODES), slice(MODES, P)
            cols = slice(L0, L0 + LA)
            a.activation(a1[top, :, :], e_re[top, :, cols], ACT.Copy).then_inc(s_atab, 1)
            a.activation(a2[top, :, :], e_im[top, :, cols], ACT.Copy, scale=-1.0).then_inc(s_atab, 1)
            a.activation(a1[bot, :, :], e_im[bot, :, cols], ACT.Copy).then_inc(s_atab, 1)
            a.activation(a2[bot, :, :], e_re[bot, :, cols], ACT.Copy).then_inc(s_atab, 1)
            with act.Fori(0, NGRP // 2) as it:
                act.wait_ge(s_wload, it * 16 + 5 * 16)
                a.activation(w_hi[:, bass.ds(it, 1), :], w_stage[:, :].unsqueeze(1), ACT.Copy)\
                 .then_inc(s_whi, 1)
                for u in range(2):
                    act.wait_ge(s_xst[u], it * 16 + 16)
                    for n in range(2):
                        act.wait_ge(s_xmm, it * 4 + 2 * u + n + 4)
                        a.activation(x_stage[u][:, n * 512:(n + 1) * 512], bank[2 * u + n][:, :], ACT.Copy)\
                         .then_inc(s_xev, 1)

            with act.Fori(0, BATCH // SB) as i:
                act.wait_ge(s_pj, i * 14 + 1)
                for n in range(2 * SB):
                    b, half = n // 2, n % 2
                    act.wait_ge(s_tp, i * (2 * SB) + n + 9)
                    a.activation(xt_hi[:, half * 4:half * 4 + 4, b * P:(b + 1) * P],
                                 bank[TBANK[n % 4]][:, :].rearrange("p (k t) -> p k t", k=4), ACT.Copy)\
                     .then_inc(s_thi, 1)
                stores = [0] * 4
                for t in range(14):
                    act.wait_ge(s_pj, i * 14 + t + 2)
                    src = bank[2 + t % 4]
                    if t < 10:
                        act.wait_ge(s_qst[t % 4], i * (16 * SLOT_STORES[t % 4]) + 16 * (stores[t % 4] + 1))
                        stores[t % 4] += 1 if t < GG else 3
                        if t in (4, 5):
                            act.wait_ge(s_kst, i * (16 * K_STORES * GG) + 16 * K_STORES * (t - 3))
                        a.activation(hi_stage[t % 4][:, :], src[:, :], ACT.Copy)
                        a.activation(bf_stage[t % 4][:, :], src[:, :], ACT.Copy).then_inc(s_pja, 1)
                    else:
                        a.activation(v_all[:, bass.ds(i * SB + (t - 10), 1), :],
                                     src[:, 0:NG * HD].unsqueeze(1), ACT.Copy).then_inc(s_pja, 1)

            def values_of(b, slot, group):
                after(act, s_pv, b * 2 - 2)
                cols = slice(group * HD, (group + 1) * HD) if isinstance(group, int) else \
                    bass.ds(group * HD, HD)
                a.activation(v_tok[slot][:, :, 0:HD], v_all[:, slot * NG:(slot + 1) * NG, cols], ACT.Copy)\
                 .then_inc(s_vt, 1)

            def keys(b, gg, uses):
                act.wait_ge(s_qk[gg], uses)
                after(act, s_sk, b * 8 - 4 + gg * GJ)
                a.activation(k_r[gg][:, :, :], k_load[gg][:, :, :], ACT.Copy).then_inc(s_kc, 1)

            def queries(b, gg, j):
                after(act, s_sk, b * 8 + gg * GJ + j - 1)
                a.activation(q_r[j % 2][:, :], q_load[gg][:, j, :], ACT.Copy).then_inc(s_qc, 1)

            def exponentials(b, gg, tiles=range(GJ)):
                if 0 in tiles:
                    after(act, s_pv, b * 2 - 1 + gg)
                for j in tiles:
                    act.wait_ge(s_sk, b * 8 + gg * GJ + j + 1)
                    a.activation(p_t[gg][:, j, :], bank[4 + j % 2][:, :], ACT.Exp, scale=SCALE)\
                     .then_inc(s_pe, 1)
                    if j + 2 < GJ:
                        queries(b, gg, j + 2)

            def operands(b, gg):
                keys(b, gg, b * 96 + 96)
                queries(b, gg, 0)
                queries(b, gg, 1)

            def context_hi(b, slot, gg):
                act.wait_ge(s_nrm, b * 2 + gg + 1)
                after(act, s_y, b * 2 - 2)
                a.activation(o_hi[slot][:, gg * 512:(gg + 1) * 512], o_t[gg][:, :], ACT.Copy)\
                 .then_inc(s_ohi, 1)

            def step(b, slot, group=None):
                if has(b):
                    operands(b, 0)
                    exponentials(b, 0, (0, 1))
                if has(b - 2):
                    act.wait_ge(s_nmr, b - 1)
                    after(act, s_ht, b * 2 - 4)
                    a.activation(hn[:, :], h2[slot][:, :], ACT.Identity, bias=nmr2[slot][:, 0:1],
                                 scale=rstd2[slot][:, 0:1]).then_inc(s_hn, 1)
                if has(b):
                    exponentials(b, 0, (2, 3))
                if isinstance(b, int) and b == -1:
                    for k in range(KD):
                        act.wait_ge(s_wol[k % 2], 16 * (k // 2 + 1))
                        a.activation(w_hi[:, k, :], y_out[k % 2][:, :], ACT.Copy).then_inc(s_whi, 1)
                if has(b - 2):
                    after(act, s_rt, b - 2)
                    for half in range(2):
                        act.wait_ge(s_ht, b * 2 + half - 3)
                        a.activation(hn_t[:, half * 4:half * 4 + 4, :],
                                     bank[4 + half][:, :].rearrange("p (k t) -> p k t", k=4), ACT.Copy)\
                         .then_inc(s_hte, 1)
                if has(b - 1):
                    context_hi(b - 1, 1 - slot, 1)
                if has(b):
                    operands(b, 1)
                if has(b + 1):
                    values_of(b + 1, 1 - slot, (b + 1) // 2 if group is None else group)
                if has(b):
                    exponentials(b, 1, (0, 1))
                if has(b - 2):
                    act.wait_ge(s_lg, b - 1)
                    a.activation(expd[:, :], logit[:, :], ACT.Exp, bias=neg_top[:, 0:1],
                                 accum_out=zsum[:, 0:1]).then_inc(s_ex, 1)
                if has(b):
                    exponentials(b, 1, (2, 3))
                    context_hi(b, slot, 0)
                if has(b - 2):
                    act.wait_ge(s_wt, b - 1)
                    a.activation(w_aug_t[:, :], bank[5][0:NE + 1, 0:P], ACT.Copy).then_inc(s_wte, 1)

            for b in range(-1, STEADY):
                step(b, b % 2)
            with act.Fori(0, N_STEADY) as pr:
                for u in range(2):
                    step(pr * 2 + (STEADY + u), (STEADY + u) % 2, pr + (STEADY + u + 1) // 2)
            for b in range(STEADY + 2 * N_STEADY, BATCH + 3):
                step(b, b % 2)

        @block.vector
        def _(dve):
            v = nc.vector
            dve.sem_inc(s_fac, 2)
            dve.sem_inc(s_tlo, 4)
            ch = Chain(dve, s_dve)
            tt, stt, ts = v.tensor_tensor, v.scalar_tensor_tensor, v.tensor_scalar
            s = {n: t[:, :] for n, t in sm.items()}
            dve.wait_ge(s_steps, 3)
            ch.mark(v.tensor_copy(steps[:, :], steps_i[:, :]))
            dve.wait_ge(s_dt, 2)
            ch.mark(stt(s["ar"], s["em"], -1.0, s["dt"], ALU.mult, ALU.mult))
            ch.link(tt(s["ai"], s["aim"], s["dt"], ALU.mult))
            st_b = bcast(steps[:, :], 1, T)
            ch.link(tt(th, bcast(s["ai"], 2, NSTEP), st_b, ALU.mult))
            ch.link(ts(kk, th, float(1.0 / TWO_PI), ROUND, ALU.mult, ALU.add))
            ch.link(ts(kk, kk, ROUND, None, ALU.subtract))
            for c in (C1, C2, C3):
                ch.link(stt(th, kk, -c, th, ALU.mult, ALU.add))
            ts(th, th, PI_IN, -PI_IN, ALU.min, ALU.max).then_inc(s_angle, 1)
            dve.wait_ge(s_angle, 1)
            stt(kk, th, -1.0, th, ALU.mult, ALU.min).then_inc(s_angle, 1)

            def w_low(dst, chunk, high):
                tt(dst, chunk, high, ALU.subtract).then_inc(s_wlo, 1)

            for k in range(KD // 2):
                dve.wait_ge(s_whi, k + 1)
                w_low(kv_lo[:, k, :], w_stage[:, :], kv_hi[:, k, :].bitcast(F32))
            ch.mark(tt(s["den"], s["em"], s["em"], ALU.mult))
            ch.link(tt(s["m"], s["aim"], s["aim"], ALU.mult))
            ch.link(tt(s["den"], s["den"], s["m"], ALU.add))
            ch.link(v.reciprocal(s["den"], s["den"]))
            ch.mark(stt(s["nr"], s["em"], -2.0, s["den"], ALU.mult, ALU.mult))
            ch.mark(stt(s["ni"], s["aim"], -2.0, s["den"], ALU.mult, ALU.mult))
            dve.wait_ge(s_trig, 2)
            tt(th, bcast(s["ar"], 2, NSTEP), st_b, ALU.mult).then_inc(s_decay, 1)
            ch.link(stt(s["q2"], s["sh"], 2.0, s["sh"], ALU.mult, ALU.mult))
            ch.mark(ts(s["m"], s["q2"], -1.0, 1.0, ALU.mult, ALU.add))
            dve.wait_ge(s_mag, 2)
            ch.link(stt(s["xr"], kk[:, :, J_ONE], 1.0, s["tnh"], ALU.add, ALU.mult))
            ch.link(tt(s["xr"], s["xr"], s["m"], ALU.mult))
            ch.mark(tt(s["xr"], s["xr"], s["q2"], ALU.subtract))
            dve.wait_ge(s_trig, 3)
            tt(e_re[:, :, :], e_re[:, :, :], kk, ALU.mult).then_inc(s_dve, 1)
            ch.k += 1
            ch.link(tt(e_im[:, :, :], e_im[:, :, :], kk, ALU.mult))
            v.tensor_copy(s["sh"], e_im[:, :, J_ONE]).then_inc(s_etab, 1)
            dve.wait_ge(s_etab, 1)
            xi = s["sh"]

            def cmul(zr, zi, ar_, ai_, br_, bi_, t):
                ch.mark(tt(zr, ar_, br_, ALU.mult))
                ch.link(tt(t, ai_, bi_, ALU.mult))
                ch.mark(tt(zr, zr, t, ALU.subtract))
                ch.link(tt(zi, ar_, bi_, ALU.mult))
                ch.link(tt(t, ai_, br_, ALU.mult))
                ch.link(tt(zi, zi, t, ALU.add))

            cmul(s["yr"], s["yi"], s["xr"], xi, s["nr"], s["ni"], s["m"])
            cmul(s["fr"], s["fi"], s["yr"], s["yi"], s["bre"], s["bim"], s["m"])
            ch.mark(ts(s["nfr"], s["fr"], -1.0, None, ALU.mult))
            ch.wait()
            z = [work[:, n, :].rearrange("p (h l) -> p h l", l=L0) for n in range(4)]
            e0r, e0i = e_re[:, :, 0:L0], e_im[:, :, 0:L0]
            ch.mark(tt(z[0], bcast(s["fr"], 2, L0), e0r, ALU.mult))
            ch.mark(tt(z[1], bcast(s["fi"], 2, L0), e0i, ALU.mult))
            ch.mark(tt(z[2], bcast(s["nfr"], 2, L0), e0i, ALU.mult))
            ch.link(tt(z[3], bcast(s["fi"], 2, L0), e0r, ALU.mult))
            top, bot = slice(0, MODES), slice(MODES, P)
            ch.mark(tt(g1[top, :, :], z[0][top], z[1][top], ALU.subtract))
            ch.mark(tt(g2[top, :, :], z[2][top], z[3][top], ALU.subtract))
            ch.mark(tt(g1[bot, :, :], z[2][bot], z[3][bot], ALU.subtract))
            ch.link(tt(g2[bot, :, :], z[1][bot], z[0][bot], ALU.subtract))
            dve.wait_ge(s_atab, 4)
            dve.wait_ge(s_c, 64)

            base = ch.k
            with dve.Fori(0, NGRP // 2) as it:
                lc = Chain(dve, s_dve, it * 6 + base)
                for u in range(2):
                    hs = bass.ds(it * (2 * HG) + u * HG, HG)
                    dve.wait_ge(s_xmm, it * 4 + 2 * u + 1)
                    dve.wait_ge(s_fac, it * 4 + 2 * u + 1)
                    v4 = "p (h a b) -> p h a b"
                    e1 = e1_slot[u].rearrange(v4, h=HG, a=LA)
                    t2 = t2_tmp.rearrange(v4, h=HG, a=LA)
                    b1 = bcast(e_re[:, hs, L0 + LA:NSTEP], 2, LA)
                    b2 = bcast(e_im[:, hs, L0 + LA:NSTEP], 2, LA)
                    lc.mark(tt(t2, bcast(a2[:, hs, :], 3, LB), b2, ALU.mult))
                    lc.mark(tt(e1, bcast(a1[:, hs, :], 3, LB), b1, ALU.mult))
                    p1 = p1_slot[u].rearrange(v4, h=HG, a=BATCH)
                    p2 = p2_slot[u].rearrange(v4, h=HG, a=BATCH)
                    lc.mark(tt(p1, bcast(c_re[:, hs, :], 3, L0), bcast(g1[:, hs, :], 2, BATCH), ALU.mult))
                    dve.wait_ge(s_dve, it * 6 + (base + 3 * u + 2))
                    tt(e1_slot[u], e1_slot[u], t2_tmp, ALU.add).then_inc(s_fac, 1)
                    tt(p2, bcast(c_im[:, hs, :], 3, L0), bcast(g2[:, hs, :], 2, BATCH), ALU.mult)\
                        .then_inc(s_fac, 1)
                dve.wait_ge(s_whi, it + 5)
                w_low(w_lo[:, bass.ds(it, 1), :], w_stage[:, :].unsqueeze(1), w_hi[:, bass.ds(it, 1), :].bitcast(F32))
                assert lc.k == 6
            ch.k = base + 6 * (NGRP // 2)

            def rsqrt(c, y, var_in, var, i32, tmp):
                c.link(ts(var, var_in, EPS, None, ALU.add))
                c.link(ts(i32, var.bitcast(I32), 1, None, ALU.logical_shift_right))
                c.link(ts(y.bitcast(I32), i32, -1.0, RSQRT_MAGIC, ALU.mult, ALU.add))
                for _ in range(3):
                    c.link(tt(tmp, y, y, ALU.mult))
                    c.link(stt(tmp, tmp, -0.5, var, ALU.mult, ALU.mult))
                    c.link(stt(y, tmp, 1.5, y, ALU.add, ALU.mult))

            dve.wait_ge(s_const, N_CONST)
            ch.mark(v.tensor_reduce(in_place[:, :], ident[:, :].rearrange("p (a r) -> p r a", r=REP),
                                    AX.X, ALU.add))
            ch.link(v.tensor_reduce(in_group[:, :],
                                    ident[:, :].rearrange("p (q g r) -> p g q r", q=4, r=REP),
                                    AX.XY, ALU.add))
            ch.wait()
            ch.mark(ts(group_sel[:, :, :], bcast(in_group[:, :], 2, P), 0.25, None, ALU.mult))
            base_b = ch.k
            PER_B = SB + 1 + 12
            with dve.Fori(0, BATCH // SB) as i:
                c = Chain(dve, s_dve, i * PER_B + base_b)
                for n in range(SB):
                    dve.wait_ge(s_xld[n], i * 16 + 16)
                    v.bn_stats(bst[:, n, 0:6], x_tok[n][:, 0:512])
                    c.mark(v.bn_stats(bst[:, n, 6:12], x_tok[n][:, 512:1024]))
                c.wait()
                carry_dve()
                for n in range(SB):
                    ins = v.bn_aggr(bmv[:, n, :], bst[:, n, :])
                c.link(ins)
                rsqrt(c, bvr[:, 1, :], bmv[:, :, 1], bvr[:, 0, :], bvr[:, 2, :].bitcast(I32), bvr[:, 3, :])
                for n in range(SB):
                    ts(x_tok[n][:, :], x_tok[n][:, :], bmv[:, n, 0:1], bvr[:, 1, n:n + 1],
                       ALU.subtract, ALU.mult).then_inc(s_xn, 1)
                for n in range(2 * SB):
                    b, half = n // 2, n % 2
                    dve.wait_ge(s_thi, i * (2 * SB) + n + 1)
                    part = (slice(None), slice(half * 4, half * 4 + 4), slice(b * P, (b + 1) * P))
                    tt(xt_lo[part], bank[TBANK[n % 4]][:, :].rearrange("p (k t) -> p k t", k=4),
                       xt_hi[part].bitcast(F32), ALU.subtract).then_inc(s_tlo, 1)
                for t in range(QK):
                    dve.wait_ge(s_pja, i * 14 + t + 1)
                    tt(lo_stage[t % 4][:, :], bank[2 + t % 4][:, :], hi_stage[t % 4][:, :].bitcast(F32),
                       ALU.subtract).then_inc(s_pjl, 1)
                assert c.k == PER_B, c.k
            ch.k = base_b + PER_B * (BATCH // SB)

            def maximum(b, slot, gg, j):
                dve.wait_ge(s_sq, b * 8 + gg * GJ + j + 1)
                h0 = (gg * GJ + j) * REP
                v.tensor_reduce(row_max[slot][:, 0, h0:h0 + REP],
                                bank[2 + j % 2][:, :].rearrange("p (r k) -> p r k", r=REP),
                                AX.X, ALU.max).then_inc(s_mx, 1)

            def copy_maxima(b, slot):
                dve.wait_ge(s_mx, b * 8 + 8)
                v.tensor_copy(row_max[slot][:, 1:4, :], bcast(row_max[slot][:, 0, :], 1, 3))\
                    .then_inc(s_mc, 1)

            def shifts(b, slot):
                dve.wait_ge(s_mt, b + 1)
                stt(shift[:, :, :], bcast(bank[4][:, 0:P], 1, REP), -1.0,
                    bcast(in_place[:, :], 2, P), ALU.mult, ALU.mult).then_inc(s_sh, 1)

            def normalise(c, b, gg, between=()):
                dve.wait_ge(s_pv, b * 2 + gg + 1)
                after(dve, s_nrm, b * 2 + gg)
                between = list(between)
                pieces = len(between) or 1
                for n in range(pieces):
                    cols = slice(n * 512 // pieces, (n + 1) * 512 // pieces)
                    c.mark(v.reciprocal(rinv[:, cols], bank[7][:, cols]))
                    if between:
                        between[n]()
                c.wait()
                after(dve, s_olo, b * 2 + gg - 1)
                tt(o_t[gg][:, :], bank[6][:, :], rinv[:, :], ALU.mult).then_inc(s_nrm, 1)

            def add_residual(b, slot, n):
                dve.wait_ge(s_y, b * 2 + n + 1)
                if n == 0:
                    dve.wait_ge(s_xb, b + 1)
                    after(dve, s_fin, b - 1)
                cols = slice(n * 512, (n + 1) * 512)
                tt(h2[slot][:, cols], bank[n][:, :], x_res[slot][:, cols], ALU.add)\
                    .then_inc(s_h2 if n else s_r0, 1)

            def statistics(b, slot, n):
                dve.wait_ge(s_h2 if n else s_r0, b + 1)
                return v.bn_stats(cst[:, n * 6:n * 6 + 6], h2[slot][:, n * 512:(n + 1) * 512])

            def norm_rows(c, b, slot):
                c.link(statistics(b, slot, 1))
                carry_dve()
                c.link(v.bn_aggr(cmv[:, :], cst[:, :]))
                rsqrt(c, rstd2[slot][:, :], cmv[:, 1:2], cvr[:, 0:1], cvr[:, 2:3].bitcast(I32), cvr[:, 3:4])
                stt(nmr2[slot][:, :], cmv[:, 0:1], -1.0, rstd2[slot][:, :], ALU.mult, ALU.mult)\
                    .then_inc(s_nmr, 1)
                dve.wait_ge(s_nmr, b + 1)

            def choose(c, b):
                dve.wait_ge(s_rt, b + 1)
                c.link(tt(logit[:, :], bank[1][:, 0:NE], rb_all[:, :], ALU.add))
                carry_dve()
                c.link(v.max(ranked[:, :], logit[:, :]))
                carry_dve()
                c.mark(v.match_replace(out=struck[:, :], in_to_replace=ranked[:, :], in_values=logit[:, :],
                                       imm_value=LOWEST))
                ts(neg_top[:, :], ranked[:, 0:1], -1.0, None, ALU.mult).then_inc(s_lg, 1)
                c.wait()
                c.link(tt(chosen[:, :], struck[:, :], logit[:, :], ALU.not_equal))

            def weigh(c, b, slot):
                dve.wait_ge(s_ex, b + 1)
                c.mark(v.reciprocal(rz[:, :], zsum[:, :]))
                c.link(stt(expd[:, :], expd[:, :], 1.0, chosen[:, :], ALU.mult, ALU.mult,
                           accum_out=wsum[:, :]))
                c.link(tt(wsum[:, :], wsum[:, :], rz[:, :], ALU.mult))
                after(dve, s_wt, b)
                ts(w_aug[:, 0:NE], expd[:, :], rz[:, :], None, ALU.mult)
                tt(w_aug[:, NE:NE + 1], nmr2[slot][:, :], wsum[:, :], ALU.mult)
                ts(hscale[slot][:, :], wsum[:, :], rstd2[slot][:, :], 1.0, ALU.mult, ALU.add)\
                    .then_inc(s_wa, 1)

            def finish(b, slot):
                dve.wait_ge(s_mix, b + 1)
                dve.wait_ge(s_out[slot], out_count(b))
                for n in range(2):
                    cols = slice(n * 512, (n + 1) * 512)
                    ins = stt(y_out[slot][:, cols], h2[slot][:, cols], hscale[slot][:, :],
                              bank[2 + n][:, :], ALU.mult, ALU.add)
                ins.then_inc(s_fin, 1)

            pair_of = [None]

            def out_count(b):
                return 16 * (b // 2 + 1) if isinstance(b, int) else pair_of[0] * 16 + 16

            def step(c, b, slot):
                other = 1 - slot
                top = [lambda j=j: maximum(b + 1, other, 0, j) for j in range(GJ)] if has(b + 1) else []
                if has(b - 2):
                    add_residual(b - 2, slot, 1)
                    norm_rows(c, b - 2, slot)
                if has(b - 1):
                    normalise(c, b - 1, 1, top)
                else:
                    for f in top:
                        f()
                if isinstance(b, int) and b == -1:
                    for k in range(KD):
                        dve.wait_ge(s_whi, 12 + k + 1)
                        w_low(w_lo[:, k, :], y_out[k % 2][:, :], w_hi[:, k, :].bitcast(F32))
                    dve.wait_ge(s_tab, 64)
                if has(b - 3):
                    finish(b - 3, other)
                if has(b - 1):
                    add_residual(b - 1, other, 0)
                if has(b - 2):
                    choose(c, b - 2)
                if has(b + 1):
                    for j in range(GJ):
                        maximum(b + 1, other, 1, j)
                        if has(b - 1) and j == 1:
                            c.mark(statistics(b - 1, other, 0))
                    copy_maxima(b + 1, other)
                elif has(b - 1):
                    c.mark(statistics(b - 1, other, 0))
                if has(b - 2):
                    weigh(c, b - 2, slot)
                if has(b):
                    normalise(c, b, 0)
                if has(b + 1):
                    shifts(b + 1, other)

            PER_C = (2 + 12) + (4 + 1) + 4 + 1 + 3
            for b in range(-1, STEADY):
                step(ch, b, b % 2)
            base_c = ch.k
            with dve.Fori(0, N_STEADY) as pr:
                lc = Chain(dve, s_dve, pr * (2 * PER_C) + base_c)
                for u in range(2):
                    pair_of[0] = pr
                    step(lc, pr * 2 + (STEADY + u), (STEADY + u) % 2)
                assert lc.k == 2 * PER_C, lc.k
            ch.k = base_c + 2 * PER_C * N_STEADY
            for b in range(STEADY + 2 * N_STEADY, BATCH + 3):
                step(ch, b, b % 2)

        @block.tensor
        def _(pe):
            mm = nc.tensor.matmul
            pe.sem_inc(s_xmm, 3)
            pe.sem_inc(s_tp, 8)
            pe.sem_inc(s_pj, 1)
            with pe.Fori(0, NGRP // 2) as it:
                for u in range(2):
                    pe.wait_ge(s_fac, it * 4 + 2 * u + 4)
                    pe.wait_ge(s_xev, it * 4 + 2 * u + 1)
                    for h in range(HG):
                        dst = bank[2 * u + h // 4][:, (h % 4) * L1:(h % 4 + 1) * L1]
                        e1 = e1_slot[u][:, h * L1:(h + 1) * L1]
                        mm(dst, p1_slot[u][:, h * P:(h + 1) * P], e1, start=True, stop=False)
                        ins = mm(dst, p2_slot[u][:, h * P:(h + 1) * P], e1, start=False, stop=True)
                        if h % 4 == 3:
                            ins.then_inc(s_xmm, 1)

            def split_product(dst, parts):
                for n, (lh, ll, rh, rl) in enumerate(parts):
                    mm(dst, lh, rh, start=n == 0, stop=False)
                    mm(dst, lh, rl, start=False, stop=False)
                    ins = mm(dst, ll, rh, start=False, stop=n == len(parts) - 1)
                return ins

            def kv_cols(w, k, c0, n):
                return w[:, k // 2, (k % 2) * 512 + c0:(k % 2) * 512 + c0 + n]

            pe.wait_ge(s_const, N_CONST)
            with pe.Fori(0, BATCH // SB) as i:
                for n in range(2 * SB):
                    b, half = n // 2, n % 2
                    pe.wait_ge(s_tlo, i * (2 * SB) + n + 1)
                    if half == 0:
                        pe.wait_ge(s_xn, i * SB + b + 1)
                    for k in range(4):
                        c = (half * 4 + k) * P
                        ins = nc.tensor.transpose(bank[TBANK[n % 4]][:, k * P:(k + 1) * P],
                                                  x_tok[b][:, c:c + P], ident[:, :])
                    ins.then_inc(s_tp, 1)
                pe.wait_ge(s_tlo, i * (2 * SB) + 2 * SB + 4)
                for t in range(14):
                    dst = bank[2 + t % 4]
                    if t >= 4:
                        pe.wait_ge(s_pjl, i * QK + t - 3)
                    if t < GG:
                        ins = split_product(dst[:, :], [
                            (kv_cols(kv_hi, k, t * P, P), kv_cols(kv_lo, k, t * P, P), xt_hi[:, k, :],
                             xt_lo[:, k, :]) for k in range(KD)])
                    elif t < 10:
                        cols = slice((t - GG) * P, (t - GG + 1) * P)
                        ins = split_product(dst[:, :], [
                            (w_hi[:, k, cols], w_lo[:, k, cols], xt_hi[:, k, :], xt_lo[:, k, :])
                            for k in range(KD)])
                    else:
                        tok = slice((t - 10) * P, (t - 9) * P)
                        ins = split_product(dst[:, 0:NG * HD], [
                            (xt_hi[:, k, tok], xt_lo[:, k, tok], kv_cols(kv_hi, k, 256, 256),
                             kv_cols(kv_lo, k, 256, 256)) for k in range(KD)])
                    ins.then_inc(s_pj, 1)

            def row_tile(b, slot, gg, j, uses):
                if gg == 0 and j == 0:
                    pe.wait_ge(s_qb[slot], uses * 32)
                if gg == 1 and j == 0:
                    after(pe, s_fin, b - 3)
                after(pe, s_mx, b * 8 + gg * GJ + j - 1)
                rows = slice(j * HD, (j + 1) * HD)
                dst = bank[2 + j % 2]
                mm(dst[:, :], ident_bf[:, :], above_bf[:, :, :].rearrange("p r k -> p (r k)"),
                   start=True, stop=False, skip_group_check=True)
                for r in range(REP):
                    ins = mm(dst[:, r * P:(r + 1) * P], q_bf[slot][rows, gg * REP + r, :],
                             k_bf[slot][rows, gg, :], start=False, stop=r == REP - 1,
                             skip_group_check=True)
                ins.then_inc(s_sq, 1)

            def key_tile(b, gg, j):
                if gg == 0 and j == 0:
                    pe.wait_ge(s_sh, b + 1)
                if gg == 0 and j == 1:
                    after(pe, s_wte, b - 2)
                if gg == 1 and j == 0:
                    after(pe, s_hte, b * 2 - 2)
                after(pe, s_pe, b * 8 + gg * GJ + j - 1)
                if j == 0:
                    pe.wait_ge(s_kc, b * 2 + gg + 1)
                pe.wait_ge(s_qc, b * 8 + gg * GJ + j + 1)
                mm(bank[4 + j % 2][:, :], k_r[gg][:, j, :], q_r[j % 2][:, :], start=True, stop=False)
                mm(bank[4 + j % 2][:, :], group_sel[:, gg * GJ + j, :],
                   shift[:, :, :].rearrange("p r q -> p (r q)"), start=False, stop=True).then_inc(s_sk, 1)

            def transpose_max(b, slot):
                pe.wait_ge(s_mc, b + 1)
                after(pe, s_pe, b * 8)
                nc.tensor.transpose(bank[4][:, 0:P], row_max[slot][:, :, :].rearrange("p q h -> p (q h)"),
                                    ident[:, :]).then_inc(s_mt, 1)

            def values(b, slot, gg):
                if gg == 0:
                    pe.wait_ge(s_vt, b + 1)
                pe.wait_ge(s_msk, b * 2 + gg + 2)
                after(pe, s_nrm, b * 2 + gg)
                for j in range(GJ):
                    mm(bank[6][j * HD:(j + 1) * HD, :], v_tok[slot][:, gg * GJ + j, :], p_t[gg][:, j, :],
                       start=True, stop=True)
                for j in range(GJ):
                    ins = mm(bank[7][j * HD:(j + 1) * HD, :], ones32[:, :], p_t[gg][:, j, :],
                             start=True, stop=True)
                ins.then_inc(s_pv, 1)

            def project(b, slot, n, gg, ks=range(4)):
                if gg == 0 and 0 in ks and n == 0:
                    after(pe, s_r0, b)
                if gg == 0 and 0 in ks and n == 1 and has(b - 1):
                    pe.wait_ge(s_lg, b)
                cols = slice(n * 512, (n + 1) * 512)
                pe.wait_ge(s_olo, b * 2 + gg + 1)
                for k in ks:
                    k = gg * 4 + k
                    lhs = slice(k * P, (k + 1) * P)
                    mm(bank[n][:, :], o_hi[slot][:, lhs], w_hi[:, k, cols], start=k == 0, stop=False)
                    mm(bank[n][:, :], o_hi[slot][:, lhs], w_lo[:, k, cols], start=False, stop=False)
                    ins = mm(bank[n][:, :], o_lo[slot][:, lhs], w_hi[:, k, cols], start=False,
                             stop=k == KD - 1)
                if k == KD - 1:
                    ins.then_inc(s_y, 1)

            def transpose_rows(b):
                pe.wait_ge(s_hn, b + 1)
                if has(b + 2):
                    pe.wait_ge(s_pe, b * 8 + 20)
                for half in range(2):
                    for k in range(4):
                        c = (half * 4 + k) * P
                        ins = nc.tensor.transpose(bank[4 + half][:, k * P:(k + 1) * P], hn[:, c:c + P],
                                                  ident[:, :])
                    ins.then_inc(s_ht, 1)

            def router(b):
                pe.wait_ge(s_hte, b * 2 + 2)
                if not has(b + 1):
                    pe.wait_ge(s_h2, b + 1)
                for k in range(KD):
                    ins = mm(bank[1][:, 0:NE], hn_t[:, k, :], rw[:, k, :], start=k == 0, stop=k == KD - 1)
                ins.then_inc(s_rt, 1)

            def transpose_weights(b):
                pe.wait_ge(s_wa, b + 1)
                if has(b + 2):
                    pe.wait_ge(s_pe, b * 8 + 24)
                nc.tensor.transpose(bank[5][0:NE + 1, 0:P], w_aug[:, :], ident[:, :]).then_inc(s_wt, 1)

            def mix(b):
                pe.wait_ge(s_wte, b + 1)
                if has(b + 4):
                    pe.wait_ge(s_mx, b * 8 + 36)
                else:
                    after(pe, s_fin, b)
                for n in range(2):
                    ins = mm(bank[2 + n][:, :], w_aug_t[:, :], eb_one[:, n * 512:(n + 1) * 512],
                             start=True, stop=True)
                ins.then_inc(s_mix, 1)

            def step(b, slot, pair=None):
                other = 1 - slot
                next_uses = (b + 1) // 2 + 1 if pair is None else pair + 1

                def scores(gg):
                    for j in range(GJ):
                        if has(b):
                            key_tile(b, gg, j)
                        if has(b - 1):
                            project(b - 1, other, gg, 0, (j,))
                        if has(b + 1):
                            row_tile(b + 1, other, gg, j, next_uses)

                if isinstance(b, int) and b == 1:
                    pe.wait_ge(s_whi, 12 + KD)
                    pe.wait_ge(s_wlo, 12 + KD)
                    pe.wait_ge(s_tab, 64)
                    pe.wait_ge(s_ones, 1)
                if has(b - 1):
                    values(b - 1, other, 1)
                scores(0)
                if has(b - 3):
                    mix(b - 3)
                if has(b - 2):
                    transpose_rows(b - 2)
                if has(b - 1):
                    project(b - 1, other, 0, 1)
                if has(b - 2):
                    router(b - 2)
                scores(1)
                if has(b):
                    values(b, slot, 0)
                if has(b + 1):
                    transpose_max(b + 1, other)
                if has(b - 1):
                    project(b - 1, other, 1, 1)
                if has(b - 2):
                    transpose_weights(b - 2)

            pe.wait_ge(s_pja, 14 * (BATCH // SB))
            for b in range(-1, STEADY):
                step(b, b % 2)
            with pe.Fori(0, N_STEADY) as pr:
                for u in range(2):
                    step(pr * 2 + (STEADY + u), (STEADY + u) % 2, pr + (STEADY + u + 1) // 2)
            for b in range(STEADY + 2 * N_STEADY, BATCH + 3):
                step(b, b % 2)


def kernel(x, L0_tok_log_dt, L0_tok_B, L0_tok_inv_A_real, L0_tok_A_imag, L0_attn_Wq, L0_attn_Wkv,
           L0_attn_Wo, L0_attn_bo, L0_ffn_router_weight, L0_ffn_router_bias, L0_ffn_expert_bias):
    import concourse.bacc as bacc
    from concourse.bass_utils import run_bass_kernel_spmd

    wq = np.asarray(L0_attn_Wq).reshape(D, GG, GJ, REP, HD).transpose(0, 1, 3, 2, 4).reshape(KD, P, D)
    wkv = np.asarray(L0_attn_Wkv).reshape(D, NG, 2, HD).transpose(0, 2, 1, 3).reshape(4, 2, P, 512)
    wkv = wkv.transpose(0, 2, 1, 3).reshape(4, P, D)
    wo = np.asarray(L0_attn_Wo).reshape(GG, GJ, REP, HD, D).transpose(0, 2, 1, 3, 4).reshape(KD, P, D)
    arrays = {
        "c_re_im": np.asarray(x).transpose(3, 2, 1, 0),
        "log_dt": np.asarray(L0_tok_log_dt),
        "b_re_im": np.asarray(L0_tok_B).transpose(2, 1, 0),
        "inv_a": np.asarray(L0_tok_inv_A_real).T,
        "a_imag": np.asarray(L0_tok_A_imag).T,
        "w_qkv": np.concatenate([wq, wkv]),
        "w_out": wo,
        "bo": np.asarray(L0_attn_bo),
        "router_t": np.asarray(L0_ffn_router_weight).T,
        "rbias": np.asarray(L0_ffn_router_bias),
        "ebias": np.asarray(L0_ffn_expert_bias),
    }
    arrays = {n: np.ascontiguousarray(a) for n, a in arrays.items()}
    nc = bacc.Bacc("TRN2", target_bir_lowering=False, num_devices=1)
    args = [nc.dram_tensor(n, a.shape, mybir.dt.from_np(a.dtype), kind="ExternalInput").ap()
            for n, a in arrays.items()]
    out = nc.dram_tensor("out", (BATCH, T, D), F32, kind="ExternalOutput").ap()
    build(nc, *args, out)
    r = run_bass_kernel_spmd(nc, [arrays], core_ids=[0])
    return r.results[0]["out"]
```

```python
import numpy as np
import concourse.bass as bass
from concourse import mybir
from contextlib import ExitStack

F32 = mybir.dt.float32
F32R = mybir.dt.float32r
BF16 = mybir.dt.bfloat16
I32 = mybir.dt.int32
ALU = mybir.AluOpType
ACT = mybir.ActivationFunctionType
AX = mybir.AxisListType

P = 128
BATCH, T, D = 16, 128, 1024
MODES = 64
L0, L1 = 8, 128
LA, LB = 8, 16
NSTEP = L0 + LA + LB
J_ONE = L0 + LA + 1
KD = D // P
NH, NG, HD = 32, 8, 32
REP = NH // NG
GG = 2
GJ = NG // GG
ROWS = 3 * HD
SB = 4
NE, TOPK = 64, 8
EPS = 1e-5
SCALE = 1.0 / HD ** 0.5
NEG = -1e30
LOWEST = -3e38

HG = 8
NGRP = T // HG
H_DVE = 2
T_DVE = 88
TWO_PI = 2.0 * np.pi
C1 = 6.28125
C2 = float(np.float32(round((TWO_PI - C1) * 2 ** 20) / 2 ** 20))
C3 = float(np.float32(TWO_PI - C1 - C2))
PI_IN = 3.1415925
ROUND = 1.5 * 2.0 ** 23
RSQRT_MAGIC = float(0x5F3759DF)


def bcast(ap, axis, n):
    a = ap.unsqueeze(axis)
    shape = list(a.shape)
    shape[axis] = n
    return a.broadcast_to(shape)


class Chain:

    def __init__(self, eng, sem, base=0):
        self.eng, self.sem, self.base, self.k = eng, sem, base, 0

    def mark(self, ins):
        ins.then_inc(self.sem, 1)
        self.k += 1

    def wait(self):
        self.eng.wait_ge(self.sem, self.base + self.k)

    def link(self, ins):
        self.mark(ins)
        self.wait()


def build(nc, c_re_im, log_dt, b_re_im, inv_a, a_imag, w_qkv, w_out, bo, router_t, rbias, ebias, out):
    x_scr = nc.dram_tensor("x_scratch", (BATCH * L0, T, L1), F32, kind="Internal").ap()
    q_scr = [nc.dram_tensor(f"q_scratch{n}", (BATCH, P, GG * REP, P), F32, kind="Internal").ap()
             for n in range(2)]
    k_scr = [nc.dram_tensor(f"k_scratch{n}", (NG, GJ * HD, BATCH // SB, P), F32, kind="Internal").ap()
             for n in range(2)]
    qb_scr = nc.dram_tensor("qb_scratch", (BATCH, P, GG * REP, P), BF16, kind="Internal").ap()
    kb_scr = nc.dram_tensor("kb_scratch", (NG, GJ * HD, BATCH // SB, P), BF16, kind="Internal").ap()

    es = ExitStack()
    with es:
        def sb(name, shape, dt=F32, stack=es):
            return stack.enter_context(nc.sbuf_tensor(name, shape, dt))

        def sem(name):
            return es.enter_context(nc.semaphore(name))

        w_hi = sb("w_hi", [P, KD, D], F32R)
        w_lo = sb("w_lo", [P, KD, D], F32R)
        ident = sb("ident", [P, P])
        ident_bf = sb("ident_bf", [P, P], BF16)
        above_bf = sb("above_bf", [P, P], BF16)
        ones32 = sb("ones32", [P, HD])
        half_pi = sb("half_pi", [P, 1])
        carrier = sb("carrier", [P, 2])
        in_group = sb("in_group", [P, NG])
        in_place = sb("in_place", [P, REP])
        group_sel = sb("group_sel", [P, NG, P], F32R)

        eab = ExitStack()
        kv_hi = sb("kv_hi", [P, KD // 2, D], F32R, stack=eab)
        kv_lo = sb("kv_lo", [P, KD // 2, D], F32R, stack=eab)

        ea = ExitStack()
        w_stage = sb("w_stage", [P, D], stack=ea)
        steps = sb("steps", [P, NSTEP], stack=ea)
        steps_i = sb("steps_i", [P, NSTEP], I32, stack=ea)
        e_re = sb("e_re", [P, T, NSTEP], stack=ea)
        e_im = sb("e_im", [P, T, NSTEP], stack=ea)
        a1 = sb("a1", [P, T, LA], stack=ea)
        a2 = sb("a2", [P, T, LA], stack=ea)
        g1 = sb("g1", [P, T, L0], stack=ea)
        g2 = sb("g2", [P, T, L0], stack=ea)
        c_re = sb("c_re", [P, T, BATCH], stack=ea)
        c_im = sb("c_im", [P, T, BATCH], stack=ea)
        work = sb("work", [P, 9, D], stack=ea)
        th = work[:, 0:4, :].rearrange("p a (b j) -> p (a b) j", j=NSTEP)
        kk = work[:, 4:8, :].rearrange("p a (b j) -> p (a b) j", j=NSTEP)
        e1_slot = [work[:, 0, :], work[:, 1, :]]
        p1_slot = [work[:, 2, :], work[:, 3, :]]
        p2_slot = [work[:, 4, :], work[:, 5, :]]
        t2_tmp = work[:, 6, :]
        x_stage = [work[:, 7, :], work[:, 8, :]]
        names = ["ldt", "inva", "aim", "bre", "bim", "dt", "em", "ar", "ai", "sh", "tnh", "q2", "xr",
                 "den", "ni", "nr", "yr", "yi", "fr", "fi", "nfr", "m"]
        room = [t.rearrange("p (n t) -> p n t", t=T) for t in
                (work[:, 8, :], g1[:, :, :].rearrange("p t l -> p (t l)"),
                 g2[:, :, :].rearrange("p t l -> p (t l)"))]
        sm = {n: room[k // L0][:, k % L0, :] for k, n in enumerate(names)}
        ea.close()

        eb = ExitStack()
        v_all = sb("v_all", [P, BATCH, NG * HD], stack=eb)
        x_tok = [sb(f"x_tok{n}", [P, D], stack=eb) for n in range(SB)]
        xt_hi = sb("xt_hi", [P, KD, SB * P], F32R, stack=eb)
        xt_lo = sb("xt_lo", [P, KD, SB * P], F32R, stack=eb)
        hi_stage = [sb(f"hi_stage{n}", [P, SB * P], F32R, stack=eb) for n in range(4)]
        lo_stage = [sb(f"lo_stage{n}", [P, SB * P], stack=eb) for n in range(4)]
        bf_stage = [sb(f"bf_stage{n}", [P, SB * P], BF16, stack=eb) for n in range(4)]
        bst = sb("bst", [P, SB, 12], stack=eb)
        bmv = sb("bmv", [P, SB, 2], stack=eb)
        bvr = sb("bvr", [P, 4, SB], stack=eb)
        eb.close()
        eab.close()

        ec = ExitStack()
        p_t = [sb(f"p_t{n}", [P, GJ, REP * P], stack=ec) for n in range(2)]
        o_hi = [sb(f"o_hi{n}", [P, D], F32R, stack=ec) for n in range(2)]
        o_lo = [sb(f"o_lo{n}", [P, D], F32R, stack=ec) for n in range(2)]
        sb("v_all_place", [P, BATCH, NG * HD], stack=ec)
        q_bf = [sb(f"q_bf{n}", [P, GG * REP, P], BF16, stack=ec) for n in range(2)]
        k_bf = [sb(f"k_bf{n}", [P, GG, P], BF16, stack=ec) for n in range(2)]
        q_load, k_load = [], []
        for n in range(GG):
            q_load.append(sb(f"q_load{n}", [ROWS, GJ, REP * P], stack=ec))
            k_load.append(sb(f"k_load{n}", [ROWS, GJ, P], stack=ec))
        q_r = [sb(f"q_r{n}", [ROWS, REP * P], F32R, stack=ec) for n in range(2)]
        k_r = [sb(f"k_r{n}", [ROWS, GJ, P], F32R, stack=ec) for n in range(GG)]
        v_tok = [sb(f"v_tok{n}", [P, NG, HD], stack=ec) for n in range(2)]
        o_t = [sb(f"o_t{n}", [P, REP * P], stack=ec) for n in range(2)]
        rinv = [sb(f"rinv{n}", [P, REP * P], stack=ec) for n in range(2)]
        shift = sb("shift", [P, REP, P], F32R, stack=ec)
        row_max = sb("row_max", [P, 4, NH], stack=ec)
        x_res = [sb(f"x_res{n}", [P, D], stack=ec) for n in range(2)]
        h2 = [sb(f"h2_{n}", [P, D], stack=ec) for n in range(2)]
        hn = sb("hn", [P, D], stack=ec)
        hn_t = sb("hn_t", [P, KD, P], stack=ec)
        y_out = [sb(f"y_out{n}", [P, D], stack=ec) for n in range(2)]
        rw = sb("rw", [P, KD, NE], stack=ec)
        rb_all = sb("rb_all", [P, NE], stack=ec)
        eb_place = sb("eb_one", [P, D], stack=ec)
        eb_one = eb_place[0:NE + 1, :]
        bo_all = sb("bo_all", [P, D], stack=ec)
        cst = sb("cst", [P, 12], stack=ec)
        cmv = sb("cmv", [P, 2], stack=ec)
        cvr = sb("cvr", [P, 4], stack=ec)
        rstd2 = [sb(f"rstd2_{n}", [P, 1], stack=ec) for n in range(2)]
        nmr2 = [sb(f"nmr2_{n}", [P, 1], stack=ec) for n in range(2)]
        logit = sb("logit", [P, NE], stack=ec)
        ranked = sb("ranked", [P, TOPK], stack=ec)
        struck = sb("struck", [P, NE], stack=ec)
        neg_top = sb("neg_top", [P, 1], stack=ec)
        expd = sb("expd", [P, NE], stack=ec)
        zsum = sb("zsum", [P, 1], stack=ec)
        chosen = sb("chosen", [P, NE], stack=ec)
        wsum = sb("wsum", [P, 1], stack=ec)
        rz = sb("rz", [P, 1], stack=ec)
        w_aug = sb("w_aug", [P, NE + 1], stack=ec)
        w_aug_t = sb("w_aug_t", [NE + 1, P], stack=ec)
        hscale = [sb(f"hscale{n}", [P, 1], stack=ec) for n in range(2)]
        ec.close()
        wo_stage = [y_out[0][:, :], y_out[1][:, :], bo_all[:, :], eb_place[:, :], hn[:, :],
                    hn_t[:, :, :].rearrange("p k t -> p (k t)"), y_out[0][:, :], y_out[1][:, :]]
        WO_AHEAD = 4

        bank = [es.enter_context(nc.psum_tensor(f"bank{n}", [P, 512], F32)) for n in range(8)]

        s_par = sem("s_par")
        s_bpar = sem("s_bpar")
        s_pdecay = sem("s_pdecay")
        s_petab = sem("s_petab")
        s_c = sem("s_c")
        s_const = sem("s_const")
        s_steps = sem("s_steps")
        s_dt = sem("s_dt")
        s_angle = sem("s_angle")
        s_trig = sem("s_trig")
        s_decay = sem("s_decay")
        s_mag = sem("s_mag")
        s_etab = sem("s_etab")
        s_atab = sem("s_atab")
        s_wload = sem("s_wload")
        s_whi = sem("s_whi")
        s_wlo = sem("s_wlo")
        s_gtab = sem("s_gtab")
        s_fac = sem("s_fac")
        s_share = sem("s_share")
        s_xmm = sem("s_xmm")
        s_xev = sem("s_xev")
        s_xst = [sem(f"s_xst{n}") for n in range(2)]
        s_dve = sem("s_dve")
        s_xld = [sem(f"s_xld{n}") for n in range(SB)]
        s_xn = sem("s_xn")
        s_tp = sem("s_tp")
        s_thi = sem("s_thi")
        s_tlo = sem("s_tlo")
        s_pj = sem("s_pj")
        s_pja = sem("s_pja")
        s_pjl = sem("s_pjl")
        s_qst = [sem(f"s_qst{n}") for n in range(4)]
        s_tab = sem("s_tab")
        s_wol = [sem(f"s_wol{n}") for n in range(KD)]
        s_qk = [sem(f"s_qk{n}") for n in range(GG)]
        s_qc = sem("s_qc")
        s_kc = sem("s_kc")
        s_rld = [sem(f"s_rld{n}") for n in range(2)]
        s_qb = [sem(f"s_qb{n}") for n in range(2)]
        s_vt = sem("s_vt")
        s_sq = sem("s_sq")
        s_mx = sem("s_mx")
        s_mc = sem("s_mc")
        s_mt = sem("s_mt")
        s_sh = sem("s_sh")
        s_sk = sem("s_sk")
        s_pe = sem("s_pe")
        s_msk = sem("s_msk")
        s_pv = sem("s_pv")
        s_cv = sem("s_cv")
        s_nrm = sem("s_nrm")
        s_ohi = sem("s_ohi")
        s_olo = sem("s_olo")
        s_xb = sem("s_xb")
        s_y = sem("s_y")
        s_r0 = sem("s_r0")
        s_h2 = sem("s_h2")
        s_nmr = sem("s_nmr")
        s_hn = sem("s_hn")
        s_ht = sem("s_ht")
        s_hte = sem("s_hte")
        s_rt = sem("s_rt")
        s_lg = sem("s_lg")
        s_ex = sem("s_ex")
        s_wa = sem("s_wa")
        s_wt = sem("s_wt")
        s_wte = sem("s_wte")
        s_mix = sem("s_mix")
        s_fin = sem("s_fin")
        s_out = [sem(f"s_out{n}") for n in range(2)]
        s_ones = sem("s_ones")

        s_carry = sem("s_carry")
        s_kst = sem("s_kst")
        SLOT_STORES = [sum(1 if t < GG else 3 for t in range(10) if t % 4 == n) for n in range(4)]
        K_STORES = 3 * GJ - 1
        QK = GG + GG * REP
        TBANK = [0, 1, 6, 7]
        N_CONST = 8

        def after(eng, semaphore, count):
            if not (isinstance(count, int) and count <= 0):
                eng.wait_ge(semaphore, count)

        STEADY = 3
        N_STEADY = (BATCH - 1 - STEADY) // 2

        def has(b):
            return not isinstance(b, int) or 0 <= b < BATCH

        def carry_dve():
            nc.vector.tensor_copy(carrier[:, 0:1], ones32[:, 0:1])

        def carry_pool():
            nc.gpsimd.tensor_tensor(carrier[:, 1:2], ones32[:, 0:1], ones32[:, 0:1], ALU.mult)

        block = es.enter_context(nc.Block())

        @block.sync
        def _(sp):
            sp.dma_start(sm["ldt"][:, :], log_dt.rearrange("(a h) -> a h", a=1).broadcast_to([P, T]))\
              .then_inc(s_par, 16)
            for half in (0, MODES):
                rows = slice(half, half + MODES)
                sp.dma_start(sm["inva"][rows, :], inv_a).then_inc(s_par, 16)
                sp.dma_start(sm["aim"][rows, :], a_imag).then_inc(s_par, 16)
            for half in (0, MODES):
                rows = slice(half, half + MODES)
                sp.dma_start(sm["bre"][rows, :], b_re_im[0]).then_inc(s_bpar, 16)
                sp.dma_start(sm["bim"][rows, :], b_re_im[1]).then_inc(s_bpar, 16)
            for k in range(8, 12):
                if k > 8:
                    sp.wait_ge(s_whi, k - 8)
                    sp.wait_ge(s_wlo, k - 8)
                sp.dma_start(w_stage[:, :], w_qkv[k]).then_inc(s_wload, 16)
                if k == 8:
                    for half in (0, MODES):
                        rows = slice(half, half + MODES)
                        sp.dma_start(c_re[rows, :, :], c_re_im[0]).then_inc(s_c, 16)
                        sp.dma_start(c_im[rows, :, :], c_re_im[1]).then_inc(s_c, 16)
            for u in range(2):
                sp.sem_inc(s_xst[u], 16)
                sp.sem_inc(s_out[u], 16)
            def load_wq(k):
                sp.wait_ge(s_whi, k + 4)
                sp.wait_ge(s_wlo, k + 4)
                sp.dma_start(w_stage[:, :], w_qkv[k]).then_inc(s_wload, 16)

            def store_x(it, u):
                sp.wait_ge(s_xev, it * 4 + 2 * u + 5)
                sp.dma_start(x_scr[:, bass.ds(it * (2 * HG) + u * HG, HG), :],
                             x_stage[u].rearrange("p (h l) -> p h l", h=HG)).then_inc(s_xst[u], 16)

            load_wq(0)
            with sp.Fori(0, NGRP // 2 - 1) as it:
                store_x(it, 0)
                load_wq(it + 1)
                store_x(it, 1)
            for u in range(2):
                store_x(NGRP // 2 - 1, u)
            for u in range(2):
                sp.wait_ge(s_xst[u], 16 * (NGRP // 2 + 1))
            sp.wait_ge(s_xld[SB - 1], 16)
            for k in range(WO_AHEAD):
                sp.dma_start(wo_stage[k], w_out[k]).then_inc(s_wol[k], 16)
            for n in range(4):
                sp.sem_inc(s_qst[n], 16)
            with sp.Fori(0, BATCH // SB) as i:
                for t in range(GG + GG * REP):
                    sp.wait_ge(s_pjl, i * QK + t + 1)
                    for stage, ks, qs in ((hi_stage, k_scr[0], q_scr[0]), (lo_stage, k_scr[1], q_scr[1]),
                                          (bf_stage, kb_scr, qb_scr)):
                        src = stage[t % 4][:, :].rearrange("p (s t) -> p s t", s=SB)
                        if stage is hi_stage:
                            src = src.bitcast(F32)
                        if t < GG:
                            for g in range(GJ):
                                last = g == GJ - 1 and stage is bf_stage
                                sp.dma_start(ks[t * GJ + g].rearrange("(j w) i k -> w j i k", j=GJ)
                                             [:, :, bass.ds(i, 1), :],
                                             src[g * HD:(g + 1) * HD, :, :].unsqueeze(2))\
                                  .then_inc(s_qst[t % 4] if last else s_kst, 16)
                        else:
                            sp.dma_start(qs[bass.ds(i * SB, SB), :, t - GG, :].rearrange("s p t -> p s t"),
                                         src).then_inc(s_qst[t % 4], 16)
            for n in range(4):
                sp.wait_ge(s_qst[n], 16 * (1 + SLOT_STORES[n] * (BATCH // SB)))
            sp.wait_ge(s_kst, 16 * K_STORES * GG * (BATCH // SB))

            def load_bf(b, slot, group):
                after(sp, s_sq, b * 8 - 8)
                sp.dma_start(q_bf[slot][:, :, :], qb_scr[b]).then_inc(s_qb[slot], 16)
                sp.dma_start(k_bf[slot][:, :, :], kb_scr[group][:, slot * GG:(slot + 1) * GG, :])\
                  .then_inc(s_qb[slot], 16)

            def load_unit(b, slot, gg, group):
                if not (isinstance(b, int) and b < 1):
                    sp.wait_ge(s_qc, b * 8 - 4 + gg * GJ)
                    sp.sem_inc(s_carry, 1)
                for n, (query_part, key_part) in enumerate(((0, 0), (1, 0), (0, 1))):
                    rows = slice(n * HD, (n + 1) * HD)
                    sp.dma_start(q_load[gg][rows, :, :],
                                 q_scr[query_part][b].rearrange("(j w) (g r) q -> w j g (r q)", j=GJ, g=GG)
                                 [:, :, gg, :]).then_inc(s_qk[gg], 16)
                    sp.dma_start(k_load[gg][rows, :, :],
                                 k_scr[key_part][group].rearrange("(j w) i k -> w j i k", j=GJ)
                                 [:, :, slot * GG + gg, :]).then_inc(s_qk[gg], 16)

            x_rows = x_scr.rearrange("(b m) t l -> b t m l", b=BATCH)

            def load_res(b, slot):
                after(sp, s_h2, b - 1)
                sp.dma_start(x_res[slot][:, :].rearrange("p (m l) -> p m l", m=L0), x_rows[b])\
                  .then_inc(s_rld[slot], 16)

            for b in range(2):
                load_bf(b, b, 0)
            load_unit(0, 0, 0, 0)
            sp.wait_ge(s_pja, 14 * (BATCH // SB))
            load_unit(0, 0, 1, 0)
            for k in range(WO_AHEAD, KD):
                if k >= 6:
                    sp.wait_ge(s_whi, 12 + k - 5)
                    sp.wait_ge(s_wlo, 12 + k - 5)
                sp.dma_start(wo_stage[k], w_out[k]).then_inc(s_wol[k], 16)
            sp.wait_ge(s_whi, 12 + WO_AHEAD)
            sp.wait_ge(s_wlo, 12 + WO_AHEAD)
            sp.dma_start(bo_all[:, :], bo.rearrange("(a e) -> a e", a=1).broadcast_to([P, D]))\
              .then_inc(s_tab, 16)
            sp.dma_start(rw[:, :, :], router_t.rearrange("(k p) e -> p k e", p=P)).then_inc(s_tab, 16)
            sp.dma_start(rb_all[:, :], rbias.rearrange("(a e) -> a e", a=1).broadcast_to([P, NE]))\
              .then_inc(s_tab, 16)
            sp.dma_start(eb_one[0:NE, :], ebias).then_inc(s_tab, 16)

            def step(b, slot, groups=None):
                next_group, group = groups or ((b + 1) // 2, (b + 2) // 2)
                if not isinstance(b, int) or 0 <= b < BATCH - 2:
                    load_bf(b + 2, slot, group)
                if has(b):
                    load_res(b, slot)
                if has(b) and has(b + 1):
                    load_unit(b + 1, 1 - slot, 0, next_group)
                if has(b - 3):
                    sp.wait_ge(s_fin, b - 2)
                    sp.dma_start(out[b - 3], y_out[1 - slot][:, :]).then_inc(s_out[1 - slot], 16)
                if has(b) and has(b + 1):
                    load_unit(b + 1, 1 - slot, 1, next_group)

            for b in range(-1, STEADY):
                step(b, b % 2)
            with sp.Fori(0, N_STEADY - 1) as pr:
                for u in range(2):
                    step(pr * 2 + (STEADY + u), (STEADY + u) % 2,
                         (pr + (STEADY + u + 1) // 2, pr + (STEADY + u + 2) // 2))
            for b in range(STEADY + 2 * (N_STEADY - 1), BATCH + 3):
                step(b, b % 2)
            for u in range(2):
                sp.wait_ge(s_out[u], 16 * (BATCH // 2 + 1))

        @block.gpsimd
        def _(pool):
            g = nc.gpsimd
            g.iota(steps_i[:, 0:L0], pattern=[[P, L0]], base=0, channel_multiplier=0).then_inc(s_steps, 1)
            g.iota(steps_i[:, L0:L0 + LA], pattern=[[LB, LA]], base=0, channel_multiplier=0).then_inc(s_steps, 1)
            g.iota(steps_i[:, L0 + LA:NSTEP], pattern=[[1, LB]], base=0, channel_multiplier=0)\
             .then_inc(s_steps, 1)
            g.memset(half_pi[:, :], float(np.pi / 2)).then_inc(s_const, 1)
            g.memset(ident[:, :], 0.0).then_inc(s_const, 1)
            g.memset(ident_bf[:, :], 0.0).then_inc(s_const, 1)
            g.memset(above_bf[:, :], 0.0).then_inc(s_const, 1)
            g.memset(ones32[:, :], 1.0).then_inc(s_const, 1)
            pool.wait_ge(s_const, 5)
            for m in (ident, ident_bf):
                g.affine_select(out=m[:, :], in_=m[:, :], compare_op=ALU.not_equal, fill=1.0, base=0,
                                pattern=[[-1, P]], channel_multiplier=1).then_inc(s_const, 1)
            g.affine_select(out=above_bf[:, :], in_=above_bf[:, :], compare_op=ALU.is_ge, fill=NEG,
                            base=0, pattern=[[-1, P]], channel_multiplier=1).then_inc(s_const, 1)
            part = slice(T_DVE, T)
            st = bcast(steps[:, :], 1, T - T_DVE)
            pool.wait_ge(s_angle, 2)
            pool.wait_ge(s_trig, 2)
            g.tensor_tensor(th[:, part, :], bcast(sm["ar"][:, part], 2, NSTEP), st, ALU.mult)\
             .then_inc(s_pdecay, 1)
            pool.wait_ge(s_pdecay, 1)
            pool.wait_ge(s_trig, 3)
            pool.wait_ge(s_mag, 1)
            g.tensor_tensor(e_re[:, part, :], e_re[:, part, :], kk[:, part, :], ALU.mult)\
             .then_inc(s_petab, 1)
            pool.wait_ge(s_petab, 1)
            g.tensor_tensor(e_im[:, part, :], e_im[:, part, :], kk[:, part, :], ALU.mult)\
             .then_inc(s_petab, 1)
            pool.wait_ge(s_petab, 2)
            pool.sem_inc(s_share, 1)
            pool.wait_ge(s_atab, 4)
            pool.wait_ge(s_gtab, 1)
            pool.wait_ge(s_c, 64)
            pool.wait_ge(s_const, N_CONST)
            with pool.Fori(0, NGRP // 2) as it:
                for u in range(2):
                    hs = bass.ds(it * (2 * HG) + u * HG, HG)
                    rest = bass.ds(it * (2 * HG) + (u * HG + H_DVE), HG - H_DVE)
                    v4 = "p (h a b) -> p h a b"
                    pool.wait_ge(s_fac, it * 4 + 2 * u + 3)
                    pool.wait_ge(s_xmm, it * 4 + 2 * u + 1)
                    pool.wait_ge(s_share, it * 4 + 2 * u + 1)
                    carry_pool()
                    g.tensor_tensor(t2_tmp.rearrange(v4, h=HG, a=LA), bcast(a2[:, hs, :], 3, LB),
                                    bcast(e_im[:, hs, L0 + LA:NSTEP], 2, LA), ALU.mult)\
                     .then_inc(s_share, 1)
                    pool.wait_ge(s_share, it * 4 + 2 * u + 2)
                    carry_pool()
                    g.tensor_tensor(p2_slot[u].rearrange(v4, h=HG, a=BATCH)[:, H_DVE:],
                                    bcast(c_im[:, rest, :], 3, L0), bcast(g2[:, rest, :], 2, BATCH),
                                    ALU.mult).then_inc(s_share, 1)
            for u in range(2):
                pool.wait_ge(s_xst[u], 16 * (NGRP // 2 + 1))
            x_rows = x_scr.rearrange("(b m) t l -> b t m l", b=BATCH)
            with pool.Fori(0, BATCH // SB) as i:
                for b in range(SB):
                    pool.wait_ge(s_tp, i * (2 * SB) + 2 * b + 2)
                    pool.dma_start(x_tok[b][:, :].rearrange("p (m l) -> p m l", m=L0), x_rows[i * SB + b])\
                        .then_inc(s_xld[b], 16)
            pool.sem_inc(s_msk, 1)
            for n in range(4):
                pool.wait_ge(s_qst[n], 16 * (1 + SLOT_STORES[n] * (BATCH // SB)))
            pool.wait_ge(s_pja, 14 * (BATCH // SB))
            def mask(b, gg):
                for half in range(2):
                    js = slice(half * 2, half * 2 + 2)
                    pool.wait_ge(s_pe, b * 8 + gg * GJ + half * 2 + 2)
                    pool.wait_ge(s_msk, b * 4 + gg * 2 + half + 1)
                    carry_pool()
                    view = p_t[gg][:, js, :].rearrange("p j (r q) -> p (j r) q", r=REP)
                    g.affine_select(out=view, in_=view, compare_op=ALU.is_ge, fill=0.0, base=0,
                                    pattern=[[0, 2 * REP], [1, P]], channel_multiplier=-1)\
                     .then_inc(s_msk, 1)

            def context_lo(b, slot, gg):
                pool.wait_ge(s_ohi, b * 2 + gg + 1)
                cols = slice(gg * 512, (gg + 1) * 512)
                g.tensor_tensor(o_lo[slot][:, cols], o_t[gg][:, :], o_hi[slot][:, cols].bitcast(F32),
                                ALU.subtract).then_inc(s_olo, 1)

            def step(b, slot):
                if has(b):
                    mask(b, 0)
                if has(b - 1):
                    context_lo(b - 1, 1 - slot, 1)
                if has(b):
                    mask(b, 1)
                    context_lo(b, slot, 0)
                    if isinstance(b, int) and b == 0:
                        pool.wait_ge(s_wlo, 12 + WO_AHEAD)
                        pool.wait_ge(s_olo, 1)
                        g.memset(eb_one[NE:NE + 1, :], 1.0).then_inc(s_ones, 1)
                        pool.wait_ge(s_ones, 1)
                        pool.wait_ge(s_tab, 64)
                    pool.wait_ge(s_rld[slot], loaded(b))
                    g.tensor_tensor(x_res[slot][:, :], x_res[slot][:, :], bo_all[:, :], ALU.add)\
                     .then_inc(s_xb, 1)

            pair_of_pool = [None]

            def loaded(b):
                return 16 * (b // 2 + 1) if isinstance(b, int) else pair_of_pool[0] * 16 + 16

            step(0, 0)
            with pool.Fori(0, (BATCH - 2) // 2) as pr:
                for u in range(2):
                    pair_of_pool[0] = pr + u
                    step(pr * 2 + (u + 1), 1 - u)
            for b in range(BATCH - 1, BATCH + 1):
                step(b, b % 2)

        @block.scalar
        def _(act):
            a = nc.scalar
            act.sem_inc(s_xev, 3)
            act.wait_ge(s_par, 5 * 16)
            a.activation(sm["dt"][:, :], sm["ldt"][:, :], ACT.Exp).then_inc(s_dt, 1)
            a.activation(sm["em"][:, :], sm["inva"][:, :], ACT.Exp).then_inc(s_dt, 1)

            def kv_high(k):
                act.wait_ge(s_wload, 16 * (k + 1))
                a.activation(kv_hi[:, k, :], w_stage[:, :], ACT.Copy).then_inc(s_whi, 1)

            kv_high(0)
            act.wait_ge(s_angle, 1)
            a.activation(e_im[:, :, :], th, ACT.Sin).then_inc(s_trig, 1)
            a.activation(sm["sh"][:, :], th[:, :, J_ONE], ACT.Sin, scale=0.5).then_inc(s_trig, 1)
            act.wait_ge(s_angle, 2)
            act.wait_ge(s_const, 1)
            a.activation(e_re[:, :, :], kk, ACT.Sin, bias=half_pi[:, 0:1]).then_inc(s_trig, 1)
            kv_high(1)
            act.wait_ge(s_trig, 3)
            act.wait_ge(s_decay, 1)
            act.wait_ge(s_pdecay, 1)
            a.activation(kk, th, ACT.Exp).then_inc(s_mag, 1)
            a.activation(sm["tnh"][:, :], sm["ar"][:, :], ACT.Tanh, scale=0.5).then_inc(s_mag, 1)
            kv_high(2)
            act.wait_ge(s_etab, 1)
            top, bot = slice(0, MODES), slice(MODES, P)
            cols = slice(L0, L0 + LA)
            a.activation(a1[top, :, :], e_re[top, :, cols], ACT.Copy).then_inc(s_atab, 1)
            a.activation(a2[top, :, :], e_im[top, :, cols], ACT.Copy, scale=-1.0).then_inc(s_atab, 1)
            a.activation(a1[bot, :, :], e_im[bot, :, cols], ACT.Copy).then_inc(s_atab, 1)
            a.activation(a2[bot, :, :], e_re[bot, :, cols], ACT.Copy).then_inc(s_atab, 1)
            kv_high(3)
            with act.Fori(0, NGRP // 2) as it:
                act.wait_ge(s_wload, it * 16 + 5 * 16)
                a.activation(w_hi[:, bass.ds(it, 1), :], w_stage[:, :].unsqueeze(1), ACT.Copy)\
                 .then_inc(s_whi, 1)
                for u in range(2):
                    act.wait_ge(s_xst[u], it * 16 + 16)
                    for n in range(2):
                        act.wait_ge(s_xmm, it * 4 + 2 * u + n + 4)
                        a.activation(x_stage[u][:, n * 512:(n + 1) * 512], bank[2 * u + n][:, :], ACT.Copy)\
                         .then_inc(s_xev, 1)

            with act.Fori(0, BATCH // SB) as i:
                act.wait_ge(s_pj, i * 14 + 1)
                for n in range(2 * SB):
                    b, half = n // 2, n % 2
                    act.wait_ge(s_tp, i * (2 * SB) + n + 9)
                    a.activation(xt_hi[:, half * 4:half * 4 + 4, b * P:(b + 1) * P],
                                 bank[TBANK[n % 4]][:, :].rearrange("p (k t) -> p k t", k=4), ACT.Copy)\
                     .then_inc(s_thi, 1)
                stores = [0] * 4
                for t in range(14):
                    act.wait_ge(s_pj, i * 14 + t + 2)
                    src = bank[2 + t % 4]
                    if t < 10:
                        act.wait_ge(s_qst[t % 4], i * (16 * SLOT_STORES[t % 4]) + 16 * (stores[t % 4] + 1))
                        stores[t % 4] += 1 if t < GG else 3
                        if t in (4, 5):
                            act.wait_ge(s_kst, i * (16 * K_STORES * GG) + 16 * K_STORES * (t - 3))
                        a.activation(hi_stage[t % 4][:, :], src[:, :], ACT.Copy)
                        a.activation(bf_stage[t % 4][:, :], src[:, :], ACT.Copy).then_inc(s_pja, 1)
                    else:
                        a.activation(v_all[:, bass.ds(i * SB + (t - 10), 1), :],
                                     src[:, 0:NG * HD].unsqueeze(1), ACT.Copy).then_inc(s_pja, 1)

            def values_of(b, slot, group):
                after(act, s_pv, b * 2 - 2)
                cols = slice(group * HD, (group + 1) * HD) if isinstance(group, int) else \
                    bass.ds(group * HD, HD)
                a.activation(v_tok[slot][:, :, 0:HD], v_all[:, slot * NG:(slot + 1) * NG, cols], ACT.Copy)\
                 .then_inc(s_vt, 1)

            def keys(b, gg, uses):
                act.wait_ge(s_qk[gg], uses)
                after(act, s_sk, b * 8 - 4 + gg * GJ)
                a.activation(k_r[gg][:, :, :], k_load[gg][:, :, :], ACT.Copy).then_inc(s_kc, 1)

            def queries(b, gg, j):
                after(act, s_sk, b * 8 + gg * GJ + j - 1)
                a.activation(q_r[j % 2][:, :], q_load[gg][:, j, :], ACT.Copy).then_inc(s_qc, 1)

            def exponentials(b, gg, tiles=range(GJ)):
                if 0 in tiles:
                    after(act, s_pv, b * 2 - 1 + gg)
                for j in tiles:
                    act.wait_ge(s_sk, b * 8 + gg * GJ + j + 1)
                    a.activation(p_t[gg][:, j, :], bank[4 + j % 2][:, :], ACT.Exp, scale=SCALE)\
                     .then_inc(s_pe, 1)
                    if j + 2 < GJ:
                        queries(b, gg, j + 2)

            def operands(b, gg):
                keys(b, gg, b * 96 + 96)
                queries(b, gg, 0)
                queries(b, gg, 1)

            def context(b, gg):
                act.wait_ge(s_pv, b * 2 + gg + 1)
                after(act, s_olo, b * 2 + gg - 1)
                a.activation(o_t[gg][:, :], bank[6][:, :], ACT.Copy)
                a.activation(rinv[gg][:, :], bank[7][:, :], ACT.Copy).then_inc(s_cv, 1)

            def context_hi(b, slot, gg):
                act.wait_ge(s_nrm, b * 2 + gg + 1)
                after(act, s_y, b * 2 - 2)
                a.activation(o_hi[slot][:, gg * 512:(gg + 1) * 512], o_t[gg][:, :], ACT.Copy)\
                 .then_inc(s_ohi, 1)

            def step(b, slot, group=None):
                if has(b - 1):
                    context(b - 1, 1)
                if has(b - 3):
                    act.wait_ge(s_wt, b - 2)
                    a.activation(w_aug_t[:, :], bank[5][0:NE + 1, 0:P], ACT.Copy).then_inc(s_wte, 1)
                if has(b):
                    exponentials(b, 0)
                if has(b - 1):
                    context_hi(b - 1, 1 - slot, 1)
                if has(b):
                    operands(b, 1)
                    context(b, 0)
                if has(b - 2):
                    act.wait_ge(s_nmr, b - 1)
                    after(act, s_ht, b * 2 - 4)
                    a.activation(hn[:, :], h2[slot][:, :], ACT.Identity, bias=nmr2[slot][:, 0:1],
                                 scale=rstd2[slot][:, 0:1]).then_inc(s_hn, 1)
                if has(b + 1):
                    values_of(b + 1, 1 - slot, (b + 1) // 2 if group is None else group)
                if has(b):
                    exponentials(b, 1, (0,))
                if has(b - 2):
                    after(act, s_rt, b - 2)
                    for half in range(2):
                        act.wait_ge(s_ht, b * 2 + half - 3)
                        a.activation(hn_t[:, half * 4:half * 4 + 4, :],
                                     bank[6 + half][:, :].rearrange("p (k t) -> p k t", k=4), ACT.Copy)\
                         .then_inc(s_hte, 1)
                if has(b):
                    exponentials(b, 1, (1, 2, 3))
                if has(b + 1):
                    operands(b + 1, 0)
                if has(b):
                    context_hi(b, slot, 0)
                if isinstance(b, int) and b < 1:
                    for k in range(4 * b + 4, 4 * b + 8):
                        act.wait_ge(s_wol[k], 16)
                        a.activation(w_hi[:, k, :], wo_stage[k], ACT.Copy).then_inc(s_whi, 1)
                if has(b - 2):
                    act.wait_ge(s_lg, b - 1)
                    a.activation(expd[:, :], logit[:, :], ACT.Exp, bias=neg_top[:, 0:1],
                                 accum_out=zsum[:, 0:1]).then_inc(s_ex, 1)

            for b in range(-1, STEADY):
                step(b, b % 2)
            with act.Fori(0, N_STEADY) as pr:
                for u in range(2):
                    step(pr * 2 + (STEADY + u), (STEADY + u) % 2, pr + (STEADY + u + 1) // 2)
            for b in range(STEADY + 2 * N_STEADY, BATCH + 3):
                step(b, b % 2)

        @block.vector
        def _(dve):
            v = nc.vector
            dve.sem_inc(s_fac, 4)
            dve.sem_inc(s_tlo, 4)
            ch = Chain(dve, s_dve)
            tt, stt, ts = v.tensor_tensor, v.scalar_tensor_tensor, v.tensor_scalar
            s = {n: t[:, :] for n, t in sm.items()}
            dve.wait_ge(s_steps, 3)
            ch.mark(v.tensor_copy(steps[:, :], steps_i[:, :]))
            dve.wait_ge(s_dt, 2)
            ch.mark(stt(s["ar"], s["em"], -1.0, s["dt"], ALU.mult, ALU.mult))
            ch.link(tt(s["ai"], s["aim"], s["dt"], ALU.mult))
            ch.link(tt(th, bcast(s["ai"], 2, NSTEP), bcast(steps[:, :], 1, T), ALU.mult))
            ch.link(ts(kk, th, float(1.0 / TWO_PI), ROUND, ALU.mult, ALU.add))
            ch.link(ts(kk, kk, ROUND, None, ALU.subtract))
            for c in (C1, C2, C3):
                ch.link(stt(th, kk, -c, th, ALU.mult, ALU.add))
            ts(th, th, PI_IN, -PI_IN, ALU.min, ALU.max).then_inc(s_angle, 1)
            dve.wait_ge(s_angle, 1)
            stt(kk, th, -1.0, th, ALU.mult, ALU.min).then_inc(s_angle, 1)
            part = slice(0, T_DVE)

            def w_low(dst, chunk, high):
                tt(dst, chunk, high, ALU.subtract).then_inc(s_wlo, 1)

            def kv_low(k):
                dve.wait_ge(s_whi, k + 1)
                w_low(kv_lo[:, k, :], w_stage[:, :], kv_hi[:, k, :].bitcast(F32))

            kv_low(0)
            ch.mark(tt(s["den"], s["em"], s["em"], ALU.mult))
            ch.link(tt(s["m"], s["aim"], s["aim"], ALU.mult))
            ch.link(tt(s["den"], s["den"], s["m"], ALU.add))
            ch.link(v.reciprocal(s["den"], s["den"]))
            ch.mark(stt(s["nr"], s["em"], -2.0, s["den"], ALU.mult, ALU.mult))
            ch.mark(stt(s["ni"], s["aim"], -2.0, s["den"], ALU.mult, ALU.mult))
            dve.wait_ge(s_trig, 2)
            dve.wait_ge(s_angle, 2)
            tt(th[:, part, :], bcast(s["ar"][:, part], 2, NSTEP), bcast(steps[:, :], 1, T_DVE), ALU.mult)\
                .then_inc(s_decay, 1)
            kv_low(1)
            ch.link(stt(s["q2"], s["sh"], 2.0, s["sh"], ALU.mult, ALU.mult))
            ch.mark(ts(s["m"], s["q2"], -1.0, 1.0, ALU.mult, ALU.add))
            dve.wait_ge(s_mag, 2)
            ch.link(stt(s["xr"], kk[:, :, J_ONE], 1.0, s["tnh"], ALU.add, ALU.mult))
            ch.link(tt(s["xr"], s["xr"], s["m"], ALU.mult))
            ch.mark(tt(s["xr"], s["xr"], s["q2"], ALU.subtract))
            dve.wait_ge(s_trig, 3)
            ch.mark(tt(e_re[:, part, :], e_re[:, part, :], kk[:, part, :], ALU.mult))
            ch.link(tt(e_im[:, part, :], e_im[:, part, :], kk[:, part, :], ALU.mult))
            dve.wait_ge(s_petab, 2)
            v.tensor_copy(s["sh"], e_im[:, :, J_ONE]).then_inc(s_etab, 1)
            dve.wait_ge(s_etab, 1)
            kv_low(2)
            xi = s["sh"]

            def cmul(zr, zi, ar_, ai_, br_, bi_, t):
                ch.mark(tt(zr, ar_, br_, ALU.mult))
                ch.link(tt(t, ai_, bi_, ALU.mult))
                ch.mark(tt(zr, zr, t, ALU.subtract))
                ch.link(tt(zi, ar_, bi_, ALU.mult))
                ch.link(tt(t, ai_, br_, ALU.mult))
                ch.link(tt(zi, zi, t, ALU.add))

            dve.wait_ge(s_bpar, 4 * 16)
            cmul(s["yr"], s["yi"], s["xr"], xi, s["nr"], s["ni"], s["m"])
            cmul(s["fr"], s["fi"], s["yr"], s["yi"], s["bre"], s["bim"], s["m"])
            ch.mark(ts(s["nfr"], s["fr"], -1.0, None, ALU.mult))
            ch.wait()
            z = [work[:, n, :].rearrange("p (h l) -> p h l", l=L0) for n in range(4)]
            e0r, e0i = e_re[:, :, 0:L0], e_im[:, :, 0:L0]
            ch.mark(tt(z[0], bcast(s["fr"], 2, L0), e0r, ALU.mult))
            ch.mark(tt(z[1], bcast(s["fi"], 2, L0), e0i, ALU.mult))
            ch.mark(tt(z[2], bcast(s["nfr"], 2, L0), e0i, ALU.mult))
            ch.link(tt(z[3], bcast(s["fi"], 2, L0), e0r, ALU.mult))
            top, bot = slice(0, MODES), slice(MODES, P)
            ch.mark(tt(g1[top, :, :], z[0][top], z[1][top], ALU.subtract))
            ch.mark(tt(g2[top, :, :], z[2][top], z[3][top], ALU.subtract))
            ch.mark(tt(g1[bot, :, :], z[2][bot], z[3][bot], ALU.subtract))
            ch.link(tt(g2[bot, :, :], z[1][bot], z[0][bot], ALU.subtract))
            dve.sem_inc(s_gtab, 1)
            kv_low(3)
            dve.wait_ge(s_atab, 4)
            dve.wait_ge(s_c, 64)

            base = ch.k
            with dve.Fori(0, NGRP // 2) as it:
                lc = Chain(dve, s_dve, it * 4 + base)
                for u in range(2):
                    hs = bass.ds(it * (2 * HG) + u * HG, HG)
                    few = bass.ds(it * (2 * HG) + u * HG, H_DVE)
                    dve.wait_ge(s_xmm, it * 4 + 2 * u + 1)
                    v4 = "p (h a b) -> p h a b"
                    e1 = e1_slot[u].rearrange(v4, h=HG, a=LA)
                    lc.mark(tt(e1, bcast(a1[:, hs, :], 3, LB), bcast(e_re[:, hs, L0 + LA:NSTEP], 2, LA),
                               ALU.mult))
                    p1 = p1_slot[u].rearrange(v4, h=HG, a=BATCH)
                    p2 = p2_slot[u].rearrange(v4, h=HG, a=BATCH)
                    lc.mark(tt(p1, bcast(c_re[:, hs, :], 3, L0), bcast(g1[:, hs, :], 2, BATCH), ALU.mult))
                    dve.wait_ge(s_dve, it * 4 + (base + 2 * u + 1))
                    dve.wait_ge(s_share, it * 4 + 2 * u + 2)
                    tt(e1_slot[u], e1_slot[u], t2_tmp, ALU.add).then_inc(s_fac, 1)
                    tt(p2[:, 0:H_DVE], bcast(c_im[:, few, :], 3, L0), bcast(g2[:, few, :], 2, BATCH),
                       ALU.mult).then_inc(s_fac, 1)
                dve.wait_ge(s_whi, it + 5)
                w_low(w_lo[:, bass.ds(it, 1), :], w_stage[:, :].unsqueeze(1), w_hi[:, bass.ds(it, 1), :].bitcast(F32))
                assert lc.k == 4
            ch.k = base + 4 * (NGRP // 2)

            def rsqrt(link, y, var_in, var, i32, tmp):
                link(ts(var, var_in, EPS, None, ALU.add))
                link(ts(i32, var.bitcast(I32), 1, None, ALU.logical_shift_right))
                link(ts(y.bitcast(I32), i32, -1.0, RSQRT_MAGIC, ALU.mult, ALU.add))
                for _ in range(3):
                    link(tt(tmp, y, y, ALU.mult))
                    link(stt(tmp, tmp, -0.5, var, ALU.mult, ALU.mult))
                    link(stt(y, tmp, 1.5, y, ALU.add, ALU.mult))

            dve.wait_ge(s_const, N_CONST)
            ch.mark(v.tensor_reduce(in_place[:, :], ident[:, :].rearrange("p (a r) -> p r a", r=REP),
                                    AX.X, ALU.add))
            ch.link(v.tensor_reduce(in_group[:, :],
                                    ident[:, :].rearrange("p (q g r) -> p g q r", q=4, r=REP),
                                    AX.XY, ALU.add))
            ch.wait()
            ch.mark(ts(group_sel[:, :, :], bcast(in_group[:, :], 2, P), 0.25, None, ALU.mult))
            base_b = ch.k
            PER_B = SB + 1 + 12
            with dve.Fori(0, BATCH // SB) as i:
                c = Chain(dve, s_dve, i * PER_B + base_b)
                for n in range(SB):
                    dve.wait_ge(s_xld[n], i * 16 + 16)
                    v.bn_stats(bst[:, n, 0:6], x_tok[n][:, 0:512])
                    c.mark(v.bn_stats(bst[:, n, 6:12], x_tok[n][:, 512:1024]))
                c.wait()
                carry_dve()
                for n in range(SB):
                    ins = v.bn_aggr(bmv[:, n, :], bst[:, n, :])
                c.link(ins)
                rsqrt(c.link, bvr[:, 1, :], bmv[:, :, 1], bvr[:, 0, :], bvr[:, 2, :].bitcast(I32), bvr[:, 3, :])
                for n in range(SB):
                    ts(x_tok[n][:, :], x_tok[n][:, :], bmv[:, n, 0:1], bvr[:, 1, n:n + 1],
                       ALU.subtract, ALU.mult).then_inc(s_xn, 1)
                for n in range(2 * SB):
                    b, half = n // 2, n % 2
                    dve.wait_ge(s_thi, i * (2 * SB) + n + 1)
                    part = (slice(None), slice(half * 4, half * 4 + 4), slice(b * P, (b + 1) * P))
                    tt(xt_lo[part], bank[TBANK[n % 4]][:, :].rearrange("p (k t) -> p k t", k=4),
                       xt_hi[part].bitcast(F32), ALU.subtract).then_inc(s_tlo, 1)
                for t in range(QK):
                    dve.wait_ge(s_pja, i * 14 + t + 1)
                    tt(lo_stage[t % 4][:, :], bank[2 + t % 4][:, :], hi_stage[t % 4][:, :].bitcast(F32),
                       ALU.subtract).then_inc(s_pjl, 1)
                assert c.k == PER_B, c.k
            ch.k = base_b + PER_B * (BATCH // SB)

            def maximum(b, slot, gg, j):
                dve.wait_ge(s_sq, b * 8 + gg * GJ + j + 1)
                h0 = (gg * GJ + j) * REP
                v.tensor_reduce(row_max[:, 0, h0:h0 + REP],
                                bank[2 + j % 2][:, :].rearrange("p (r k) -> p r k", r=REP),
                                AX.X, ALU.max).then_inc(s_mx, 1)

            def copy_maxima(b, slot):
                dve.wait_ge(s_mx, b * 8 + 8)
                v.tensor_copy(row_max[:, 1:4, :], bcast(row_max[:, 0, :], 1, 3))\
                    .then_inc(s_mc, 1)

            def shifts(b, slot):
                dve.wait_ge(s_mt, b + 1)
                stt(shift[:, :, :], bcast(bank[4][:, 0:P], 1, REP), -1.0,
                    bcast(in_place[:, :], 2, P), ALU.mult, ALU.mult).then_inc(s_sh, 1)

            def normalise(c, b, gg, pieces=1):
                def piece(n):
                    if n == 0:
                        dve.wait_ge(s_cv, b * 2 + gg + 1)
                    cols = slice(n * 512 // pieces, (n + 1) * 512 // pieces)
                    c.mark(v.reciprocal(rinv[gg][:, cols], rinv[gg][:, cols]))

                def product():
                    c.wait()
                    tt(o_t[gg][:, :], o_t[gg][:, :], rinv[gg][:, :], ALU.mult).then_inc(s_nrm, 1)

                return [lambda n=n: piece(n) for n in range(pieces)] + [product]

            def add_residual(b, slot, n):
                dve.wait_ge(s_y, b * 2 + n + 1)
                if n == 0:
                    dve.wait_ge(s_xb, b + 1)
                    after(dve, s_fin, b - 1)
                cols = slice(n * 512, (n + 1) * 512)
                tt(h2[slot][:, cols], bank[n][:, :], x_res[slot][:, cols], ALU.add)\
                    .then_inc(s_h2 if n else s_r0, 1)

            def statistics(b, slot, n):
                dve.wait_ge(s_h2 if n else s_r0, b + 1)
                return v.bn_stats(cst[:, n * 6:n * 6 + 6], h2[slot][:, n * 512:(n + 1) * 512])

            def norm_rows(c, b, slot, between):
                between = list(between)

                def link(ins):
                    c.mark(ins)
                    count = c.base + c.k
                    if between:
                        between.pop(0)()
                    dve.wait_ge(s_dve, count)

                link(statistics(b, slot, 1))
                carry_dve()
                link(v.bn_aggr(cmv[:, :], cst[:, :]))
                rsqrt(link, rstd2[slot][:, :], cmv[:, 1:2], cvr[:, 0:1], cvr[:, 2:3].bitcast(I32),
                      cvr[:, 3:4])
                stt(nmr2[slot][:, :], cmv[:, 0:1], -1.0, rstd2[slot][:, :], ALU.mult, ALU.mult)\
                    .then_inc(s_nmr, 1)
                dve.wait_ge(s_nmr, b + 1)
                for work_left in between:
                    work_left()

            def choose(c, b):
                dve.wait_ge(s_rt, b + 1)
                c.link(tt(logit[:, :], bank[0][:, 0:NE], rb_all[:, :], ALU.add))
                carry_dve()
                c.link(v.max(ranked[:, :], logit[:, :]))
                carry_dve()
                c.mark(v.match_replace(out=struck[:, :], in_to_replace=ranked[:, :], in_values=logit[:, :],
                                       imm_value=LOWEST))
                ts(neg_top[:, :], ranked[:, 0:1], -1.0, None, ALU.mult).then_inc(s_lg, 1)
                c.wait()
                c.link(tt(chosen[:, :], struck[:, :], logit[:, :], ALU.not_equal))

            def weigh(c, b, slot):
                dve.wait_ge(s_ex, b + 1)
                c.mark(v.reciprocal(rz[:, :], zsum[:, :]))
                c.link(stt(expd[:, :], expd[:, :], 1.0, chosen[:, :], ALU.mult, ALU.mult,
                           accum_out=wsum[:, :]))
                c.link(tt(wsum[:, :], wsum[:, :], rz[:, :], ALU.mult))
                after(dve, s_wt, b)
                ts(w_aug[:, 0:NE], expd[:, :], rz[:, :], None, ALU.mult)
                tt(w_aug[:, NE:NE + 1], nmr2[slot][:, :], wsum[:, :], ALU.mult)
                ts(hscale[slot][:, :], wsum[:, :], rstd2[slot][:, :], 1.0, ALU.mult, ALU.add)\
                    .then_inc(s_wa, 1)

            def finish(b, slot):
                dve.wait_ge(s_mix, b + 1)
                dve.wait_ge(s_out[slot], out_count(b))
                for n in range(2):
                    cols = slice(n * 512, (n + 1) * 512)
                    ins = stt(y_out[slot][:, cols], h2[slot][:, cols], hscale[slot][:, :],
                              bank[2 + n][:, :], ALU.mult, ALU.add)
                ins.then_inc(s_fin, 1)

            pair_of = [None]

            def out_count(b):
                return 16 * (b // 2 + 1) if isinstance(b, int) else pair_of[0] * 16 + 16

            def step(c, b, slot):
                other = 1 - slot
                top = [lambda j=j: maximum(b + 1, other, 0, j) for j in range(GJ)] if has(b + 1) else []
                big = normalise(c, b - 1, 1, GJ) if has(b - 1) else []
                big = [f for pair in zip(big, top) for f in pair][:2 * GJ - 2] + top[-1:] + big[-2:] \
                    if big and top else big + top
                if has(b - 2):
                    add_residual(b - 2, slot, 1)
                    norm_rows(c, b - 2, slot, big)
                else:
                    for f in big:
                        f()
                if has(b - 3):
                    finish(b - 3, other)
                low = [lambda j=j: maximum(b + 1, other, 1, j) for j in range(GJ)] if has(b + 1) else []
                part = normalise(c, b, 0, GJ) if has(b) else []
                for f in part[:2]:
                    f()
                if has(b - 1):
                    add_residual(b - 1, other, 0)
                for f in low[0:1] + part[2:3] + low[1:2] + part[3:4] + low[2:3] + part[4:] + low[3:]:
                    f()
                if has(b + 1):
                    copy_maxima(b + 1, other)
                if has(b - 1):
                    c.mark(statistics(b - 1, other, 0))
                if has(b - 2):
                    choose(c, b - 2)
                if has(b + 1):
                    shifts(b + 1, other)
                if isinstance(b, int) and b < 1:
                    for k in range(4 * b + 4, 4 * b + 8):
                        dve.wait_ge(s_whi, 12 + k + 1)
                        w_low(w_lo[:, k, :], wo_stage[k], w_hi[:, k, :].bitcast(F32))
                if isinstance(b, int) and b == 0:
                    dve.wait_ge(s_tab, 64)
                if has(b - 2):
                    weigh(c, b - 2, slot)

            PER_C = (2 + 12) + 2 * GJ + 4 + 1 + 3
            for b in range(-1, STEADY):
                step(ch, b, b % 2)
            base_c = ch.k
            with dve.Fori(0, N_STEADY) as pr:
                lc = Chain(dve, s_dve, pr * (2 * PER_C) + base_c)
                for u in range(2):
                    pair_of[0] = pr
                    step(lc, pr * 2 + (STEADY + u), (STEADY + u) % 2)
                assert lc.k == 2 * PER_C, lc.k
            ch.k = base_c + 2 * PER_C * N_STEADY
            for b in range(STEADY + 2 * N_STEADY, BATCH + 3):
                step(ch, b, b % 2)

        @block.tensor
        def _(pe):
            mm = nc.tensor.matmul
            pe.sem_inc(s_xmm, 3)
            pe.sem_inc(s_tp, 8)
            pe.sem_inc(s_pj, 1)
            with pe.Fori(0, NGRP // 2) as it:
                for u in range(2):
                    pe.wait_ge(s_fac, it * 4 + 2 * u + 6)
                    pe.wait_ge(s_share, it * 4 + 2 * u + 3)
                    pe.wait_ge(s_xev, it * 4 + 2 * u + 1)
                    for h in range(HG):
                        dst = bank[2 * u + h // 4][:, (h % 4) * L1:(h % 4 + 1) * L1]
                        e1 = e1_slot[u][:, h * L1:(h + 1) * L1]
                        mm(dst, p1_slot[u][:, h * P:(h + 1) * P], e1, start=True, stop=False)
                        ins = mm(dst, p2_slot[u][:, h * P:(h + 1) * P], e1, start=False, stop=True)
                        if h % 4 == 3:
                            ins.then_inc(s_xmm, 1)

            def split_product(dst, parts):
                for n, (lh, ll, rh, rl) in enumerate(parts):
                    mm(dst, lh, rh, start=n == 0, stop=False)
                    mm(dst, lh, rl, start=False, stop=False)
                    ins = mm(dst, ll, rh, start=False, stop=n == len(parts) - 1)
                return ins

            def kv_cols(w, k, c0, n):
                return w[:, k // 2, (k % 2) * 512 + c0:(k % 2) * 512 + c0 + n]

            pe.wait_ge(s_const, N_CONST)
            with pe.Fori(0, BATCH // SB) as i:
                for n in range(2 * SB):
                    b, half = n // 2, n % 2
                    pe.wait_ge(s_tlo, i * (2 * SB) + n + 1)
                    if half == 0:
                        pe.wait_ge(s_xn, i * SB + b + 1)
                    for k in range(4):
                        c = (half * 4 + k) * P
                        ins = nc.tensor.transpose(bank[TBANK[n % 4]][:, k * P:(k + 1) * P],
                                                  x_tok[b][:, c:c + P], ident[:, :])
                    ins.then_inc(s_tp, 1)
                pe.wait_ge(s_tlo, i * (2 * SB) + 2 * SB + 4)
                for t in range(14):
                    dst = bank[2 + t % 4]
                    if t >= 4:
                        pe.wait_ge(s_pjl, i * QK + t - 3)
                    if t < GG:
                        ins = split_product(dst[:, :], [
                            (kv_cols(kv_hi, k, t * P, P), kv_cols(kv_lo, k, t * P, P), xt_hi[:, k, :],
                             xt_lo[:, k, :]) for k in range(KD)])
                    elif t < 10:
                        cols = slice((t - GG) * P, (t - GG + 1) * P)
                        ins = split_product(dst[:, :], [
                            (w_hi[:, k, cols], w_lo[:, k, cols], xt_hi[:, k, :], xt_lo[:, k, :])
                            for k in range(KD)])
                    else:
                        tok = slice((t - 10) * P, (t - 9) * P)
                        ins = split_product(dst[:, 0:NG * HD], [
                            (xt_hi[:, k, tok], xt_lo[:, k, tok], kv_cols(kv_hi, k, 256, 256),
                             kv_cols(kv_lo, k, 256, 256)) for k in range(KD)])
                    ins.then_inc(s_pj, 1)

            def row_tile(b, slot, gg, j, uses):
                if gg == 0 and j == 0:
                    pe.wait_ge(s_qb[slot], uses * 32)
                if gg == 1 and j == 0:
                    after(pe, s_fin, b - 3)
                after(pe, s_mx, b * 8 + gg * GJ + j - 1)
                rows = slice(j * HD, (j + 1) * HD)
                dst = bank[2 + j % 2]
                mm(dst[:, :].rearrange("p (r k) -> p r k", r=REP), ident_bf[:, :], bcast(above_bf[:, :], 1, REP),
                   start=True, stop=False, skip_group_check=True)
                for r in range(REP):
                    ins = mm(dst[:, r * P:(r + 1) * P], q_bf[slot][rows, gg * REP + r, :],
                             k_bf[slot][rows, gg, :], start=False, stop=r == REP - 1,
                             skip_group_check=True)
                ins.then_inc(s_sq, 1)

            def key_tile(b, gg, j):
                if gg == 0 and j == 0:
                    pe.wait_ge(s_sh, b + 1)
                if gg == 0 and j == 1:
                    after(pe, s_wte, b - 2)
                after(pe, s_pe, b * 8 + gg * GJ + j - 1)
                if j == 0:
                    pe.wait_ge(s_kc, b * 2 + gg + 1)
                pe.wait_ge(s_qc, b * 8 + gg * GJ + j + 1)
                mm(bank[4 + j % 2][:, :], k_r[gg][:, j, :], q_r[j % 2][:, :], start=True, stop=False)
                mm(bank[4 + j % 2][:, :], group_sel[:, gg * GJ + j, :],
                   shift[:, :, :].rearrange("p r q -> p (r q)"), start=False, stop=True).then_inc(s_sk, 1)

            def transpose_max(b, slot):
                pe.wait_ge(s_mc, b + 1)
                after(pe, s_pe, b * 8)
                nc.tensor.transpose(bank[4][:, 0:P], row_max[:, :, :].rearrange("p q h -> p (q h)"),
                                    ident[:, :]).then_inc(s_mt, 1)

            def values(b, slot, gg):
                if gg == 0:
                    pe.wait_ge(s_vt, b + 1)
                else:
                    after(pe, s_hte, b * 2 - 2)
                pe.wait_ge(s_msk, b * 4 + gg * 2 + 3)
                after(pe, s_cv, b * 2 + gg)
                for j in range(GJ):
                    mm(bank[6][j * HD:(j + 1) * HD, :], v_tok[slot][:, gg * GJ + j, :], p_t[gg][:, j, :],
                       start=True, stop=True)
                for j in range(GJ):
                    ins = mm(bank[7][j * HD:(j + 1) * HD, :], ones32[:, :], p_t[gg][:, j, :],
                             start=True, stop=True)
                ins.then_inc(s_pv, 1)

            def project(b, slot, n, gg, ks=range(4)):
                if gg == 0 and 0 in ks and n == 0 and has(b - 2):
                    pe.wait_ge(s_lg, b - 1)
                if gg == 0 and 0 in ks and n == 1:
                    after(pe, s_h2, b)
                cols = slice(n * 512, (n + 1) * 512)
                pe.wait_ge(s_olo, b * 2 + gg + 1)
                for k in ks:
                    k = gg * 4 + k
                    lhs = slice(k * P, (k + 1) * P)
                    mm(bank[n][:, :], o_hi[slot][:, lhs], w_hi[:, k, cols], start=k == 0, stop=False)
                    mm(bank[n][:, :], o_hi[slot][:, lhs], w_lo[:, k, cols], start=False, stop=False)
                    ins = mm(bank[n][:, :], o_lo[slot][:, lhs], w_hi[:, k, cols], start=False,
                             stop=k == KD - 1)
                if k == KD - 1:
                    ins.then_inc(s_y, 1)

            def transpose_rows(b):
                pe.wait_ge(s_hn, b + 1)
                pe.wait_ge(s_cv, min(b * 2 + 5, BATCH * 2) if isinstance(b, int) else b * 2 + 5)
                for half in range(2):
                    for k in range(4):
                        c = (half * 4 + k) * P
                        ins = nc.tensor.transpose(bank[6 + half][:, k * P:(k + 1) * P], hn[:, c:c + P],
                                                  ident[:, :])
                    ins.then_inc(s_ht, 1)

            def router(b):
                pe.wait_ge(s_hte, b * 2 + 2)
                if has(b + 1):
                    pe.wait_ge(s_r0, b + 2)
                for k in range(KD):
                    ins = mm(bank[0][:, 0:NE], hn_t[:, k, :], rw[:, k, :], start=k == 0, stop=k == KD - 1)
                ins.then_inc(s_rt, 1)

            def transpose_weights(b):
                pe.wait_ge(s_wa, b + 1)
                if has(b + 2):
                    pe.wait_ge(s_pe, b * 8 + 24)
                nc.tensor.transpose(bank[5][0:NE + 1, 0:P], w_aug[:, :], ident[:, :]).then_inc(s_wt, 1)

            def mix(b):
                pe.wait_ge(s_wte, b + 1)
                if has(b + 4):
                    pe.wait_ge(s_mx, b * 8 + 36)
                else:
                    after(pe, s_fin, b)
                for n in range(2):
                    ins = mm(bank[2 + n][:, :], w_aug_t[:, :], eb_one[:, n * 512:(n + 1) * 512],
                             start=True, stop=True)
                ins.then_inc(s_mix, 1)

            def step(b, slot, pair=None):
                other = 1 - slot
                next_uses = (b + 1) // 2 + 1 if pair is None else pair + 1

                def scores(gg):
                    for j in range(GJ):
                        if has(b):
                            key_tile(b, gg, j)
                        if has(b + 1):
                            row_tile(b + 1, other, gg, j, next_uses)
                        if isinstance(b, int) and b == 1 and gg == 0 and j == 0:
                            pe.wait_ge(s_whi, 12 + KD)
                            pe.wait_ge(s_wlo, 12 + KD)
                            pe.wait_ge(s_tab, 64)
                            pe.wait_ge(s_ones, 1)
                        if has(b - 1):
                            project(b - 1, other, gg, 0, (j,))
                        if gg == 1 and j == 0 and has(b - 2):
                            transpose_rows(b - 2)

                if has(b - 1):
                    values(b - 1, other, 1)
                if has(b - 3):
                    transpose_weights(b - 3)
                scores(0)
                if has(b - 3):
                    mix(b - 3)
                if has(b):
                    values(b, slot, 0)
                if has(b - 1):
                    project(b - 1, other, 0, 1)
                scores(1)
                if has(b - 2):
                    router(b - 2)
                if has(b + 1):
                    transpose_max(b + 1, other)
                if has(b - 1):
                    project(b - 1, other, 1, 1)

            pe.wait_ge(s_pja, 14 * (BATCH // SB))
            for b in range(-1, STEADY):
                step(b, b % 2)
            with pe.Fori(0, N_STEADY) as pr:
                for u in range(2):
                    step(pr * 2 + (STEADY + u), (STEADY + u) % 2, pr + (STEADY + u + 1) // 2)
            for b in range(STEADY + 2 * N_STEADY, BATCH + 3):
                step(b, b % 2)


def kernel(x, L0_tok_log_dt, L0_tok_B, L0_tok_inv_A_real, L0_tok_A_imag, L0_attn_Wq, L0_attn_Wkv,
           L0_attn_Wo, L0_attn_bo, L0_ffn_router_weight, L0_ffn_router_bias, L0_ffn_expert_bias):
    import concourse.bacc as bacc
    from concourse.bass_utils import run_bass_kernel_spmd

    wq = np.asarray(L0_attn_Wq).reshape(D, GG, GJ, REP, HD).transpose(0, 1, 3, 2, 4).reshape(KD, P, D)
    wkv = np.asarray(L0_attn_Wkv).reshape(D, NG, 2, HD).transpose(0, 2, 1, 3).reshape(4, 2, P, 512)
    wkv = wkv.transpose(0, 2, 1, 3).reshape(4, P, D)
    wo = np.asarray(L0_attn_Wo).reshape(GG, GJ, REP, HD, D).transpose(0, 2, 1, 3, 4).reshape(KD, P, D)
    arrays = {
        "c_re_im": np.asarray(x).transpose(3, 2, 1, 0),
        "log_dt": np.asarray(L0_tok_log_dt),
        "b_re_im": np.asarray(L0_tok_B).transpose(2, 1, 0),
        "inv_a": np.asarray(L0_tok_inv_A_real).T,
        "a_imag": np.asarray(L0_tok_A_imag).T,
        "w_qkv": np.concatenate([wq, wkv]),
        "w_out": wo,
        "bo": np.asarray(L0_attn_bo),
        "router_t": np.asarray(L0_ffn_router_weight).T,
        "rbias": np.asarray(L0_ffn_router_bias),
        "ebias": np.asarray(L0_ffn_expert_bias),
    }
    arrays = {n: np.ascontiguousarray(a) for n, a in arrays.items()}
    nc = bacc.Bacc("TRN2", target_bir_lowering=False, num_devices=1)
    args = [nc.dram_tensor(n, a.shape, mybir.dt.from_np(a.dtype), kind="ExternalInput").ap()
            for n, a in arrays.items()]
    out = nc.dram_tensor("out", (BATCH, T, D), F32, kind="ExternalOutput").ap()
    build(nc, *args, out)
    r = run_bass_kernel_spmd(nc, [arrays], core_ids=[0])
    return r.results[0]["out"]
```
